# Optimizing a Trainium2 kernel written in Bass

```python
import numpy as np
import jax
import jax.numpy as jnp

def _softmax(x, axis=-1):
    return jax.nn.softmax(x, axis=axis)

def _gelu(x):
    return jax.nn.gelu(x, approximate=True)

def _silu(x):
    return jax.nn.silu(x)

def _sigmoid(x):
    return jax.nn.sigmoid(x)

def _layernorm(x, axis=-1, eps=1e-05):
    m = jnp.mean(x, axis=axis, keepdims=True)
    v = jnp.var(x, axis=axis, keepdims=True)
    return (x - m) / jnp.sqrt(v + eps)

def _scatter_add(tgt, idx, src, axis=0):
    return tgt.at[idx].add(src)

def _segment_sum(src, seg, n):
    return jax.ops.segment_sum(src, seg, n)
kernel_name = 'mk_gnn_resnorm_d2_gnn_r8_a3bc5e'

def setup_inputs(seed: int=0):
    np.random.seed(seed)
    _w = jnp.asarray

    def _rec_inputs():
        import jax
        import jax.numpy as jnp
        _gk = jax.random.key(seed)
        x = -6.415e-05 + 1 * jax.random.normal(jax.random.fold_in(_gk, 1), (2500, 512), jnp.float32)
        src = jax.random.randint(jax.random.fold_in(_gk, 2), (80000,), 0, 2500, jnp.int32)
        dst = jnp.minimum((2500 * jax.random.uniform(jax.random.fold_in(_gk, 3), (80000,)) ** 2.0).astype(jnp.int32), 19999)
        _o = jnp.argsort(dst, stable=True)
        src = src[_o]
        dst = dst[_o]
        edge_type_8 = jax.random.randint(jax.random.fold_in(_gk, 13), (80000,), 0, 8, jnp.int32)
        edge_weight = jax.random.uniform(jax.random.fold_in(_gk, 14), (80000,), jnp.float32, 0.0, 0.999998)
        return (x, src, dst, edge_type_8, edge_weight)
    x, src, dst, edge_type_8, edge_weight = _rec_inputs()

    def _L0_gnn_setup():
        import jax, jax.numpy as jnp
        import numpy as np
        N = 2500
        E = 20000
        D = 512
        R = 8
        key = jax.random.key(seed)
        ks = jax.random.split(key, 8)
        inp = {'input': jax.random.normal(ks[0], (N, D), dtype=jnp.float32), 'heads': jax.random.randint(ks[1], (E,), 0, N), 'tails': jax.random.randint(ks[2], (E,), 0, N), 'rel': jax.random.randint(ks[3], (E,), 0, R), 'W_self': jax.random.normal(ks[4], (D, D), dtype=jnp.float32) * 0.03, 'b_self': jnp.zeros((D,), dtype=jnp.float32), 'W_rel': jax.random.normal(ks[5], (2 * R, D, D), dtype=jnp.float32) * 0.03, 'b_rel': jnp.zeros((2 * R, D), dtype=jnp.float32)}
        return inp
    _L0_gnn_all = _L0_gnn_setup()
    _L0_gnn_in = {k: v for k, v in _L0_gnn_all.items() if k in ('W_self', 'b_self', 'W_rel', 'b_rel')}
    del _L0_gnn_all

    def _L1_gnn_setup():
        import jax, jax.numpy as jnp
        import numpy as np
        EPS = 1e-12

        def _gcn_conv(x, W, b, src, dst, w, n_nodes):
            h = x @ W
            deg = jax.ops.segment_sum(w, dst, num_segments=n_nodes)
            dinv = jnp.where(deg > 0, jax.lax.rsqrt(deg), 0.0)
            norm = dinv[src] * w * dinv[dst]
            out = jax.ops.segment_sum(h[src] * norm[:, None], dst, num_segments=n_nodes)
            return out + b
        key = jax.random.key(seed)
        ks = jax.random.split(key, 6)
        N, E, F_in, F_hid, F_out = (6250, 50000, 512, 256, 512)
        node_features = jax.random.normal(ks[0], (N, F_in), dtype=jnp.float32)
        node_features = node_features / jnp.linalg.norm(node_features, axis=-1, keepdims=True)
        edge_index = jax.random.randint(ks[1], (2, E), 0, N, dtype=jnp.int64)
        edge_weight = jax.random.uniform(ks[2], (E,), dtype=jnp.float32)
        W1 = jax.random.normal(ks[3], (F_in, F_hid), dtype=jnp.float32) / np.sqrt(F_in)
        b1 = jnp.zeros((F_hid,), dtype=jnp.float32)
        W2 = jax.random.normal(ks[4], (F_hid, F_out), dtype=jnp.float32) / np.sqrt(F_hid)
        b2 = jnp.zeros((F_out,), dtype=jnp.float32)
        return {'node_features': node_features, 'edge_index': edge_index, 'edge_weight': edge_weight, 'W1': W1, 'b1': b1, 'W2': W2, 'b2': b2}
    _L1_gnn_all = _L1_gnn_setup()
    _L1_gnn_in = {k: v for k, v in _L1_gnn_all.items() if k in ('W1', 'b1', 'W2', 'b2')}
    del _L1_gnn_all
    return {'x': x, 'src': src, 'dst': dst, 'edge_type_8': edge_type_8, 'edge_weight': edge_weight, 'L0_gnn_W_self': _L0_gnn_in['W_self'], 'L0_gnn_b_self': _L0_gnn_in['b_self'], 'L0_gnn_W_rel': _L0_gnn_in['W_rel'], 'L0_gnn_b_rel': _L0_gnn_in['b_rel'], 'L1_gnn_W1': _L1_gnn_in['W1'], 'L1_gnn_b1': _L1_gnn_in['b1'], 'L1_gnn_W2': _L1_gnn_in['W2'], 'L1_gnn_b2': _L1_gnn_in['b2']}

def reference(x, src, dst, edge_type_8, edge_weight, L0_gnn_W_self, L0_gnn_b_self, L0_gnn_W_rel, L0_gnn_b_rel, L1_gnn_W1, L1_gnn_b1, L1_gnn_W2, L1_gnn_b2):
    import jax
    import jax.numpy as jnp

    def _L0_gnn_ref(input, heads, tails, rel, W_self, b_self, W_rel, b_rel):
        import jax, jax.numpy as jnp
        import numpy as np
        N = 2500
        E = 20000
        D = 512
        R = 8
        h_self = input @ W_self.T + b_self
        H_all = jnp.einsum('rod,nd->rno', W_rel, input) + b_rel[:, None, :]
        msg_to_heads = H_all[rel, tails]
        msg_to_tails = H_all[rel + R, heads]
        agg = jax.ops.segment_sum(msg_to_heads, heads, num_segments=N) + jax.ops.segment_sum(msg_to_tails, tails, num_segments=N)
        return jax.nn.relu(h_self + agg)

    def _L1_gnn_ref(node_features, edge_index, edge_weight, W1, b1, W2, b2):
        import jax, jax.numpy as jnp
        import numpy as np
        EPS = 1e-12

        def _gcn_conv(x, W, b, src, dst, w, n_nodes):
            h = x @ W
            deg = jax.ops.segment_sum(w, dst, num_segments=n_nodes)
            dinv = jnp.where(deg > 0, jax.lax.rsqrt(deg), 0.0)
            norm = dinv[src] * w * dinv[dst]
            out = jax.ops.segment_sum(h[src] * norm[:, None], dst, num_segments=n_nodes)
            return out + b
        N = node_features.shape[0]
        loop = jnp.arange(N, dtype=edge_index.dtype)
        src = jnp.concatenate([edge_index[0], loop])
        dst = jnp.concatenate([edge_index[1], loop])
        w = jnp.concatenate([edge_weight, jnp.ones((N,), dtype=edge_weight.dtype)])
        x = _gcn_conv(node_features, W1, b1, src, dst, w, N)
        x = jax.nn.relu(x)
        x = _gcn_conv(x, W2, b2, src, dst, w, N)
        nrm = jnp.linalg.norm(x, axis=-1, keepdims=True)
        return x / jnp.maximum(nrm, EPS)
    edge_index = jnp.stack([src, dst])
    x = _layernorm(x + _L0_gnn_ref(x, src, dst, edge_type_8, L0_gnn_W_self, L0_gnn_b_self, L0_gnn_W_rel, L0_gnn_b_rel), axis=-1)
    x = _layernorm(x + _L1_gnn_ref(x, edge_index, edge_weight, L1_gnn_W1, L1_gnn_b1, L1_gnn_W2, L1_gnn_b2), axis=-1)
    return x

_drawn_inputs = setup_inputs


def setup_inputs(seed=0):
    import zlib

    import numpy as np

    out = dict(_drawn_inputs(seed))
    spreads = {'L0_gnn_b_self': (0.0, 0.358),
     'L0_gnn_b_rel': (0.0, 0.1),
     'L1_gnn_b1': (0.0, 0.654),
     'L1_gnn_b2': (0.0, 0.384)}
    factors = {'edge_weight': 8.0}
    for name, (base, spread) in spreads.items():
        noise = np.random.default_rng([zlib.crc32(name.encode()), seed]).standard_normal(out[name].shape)
        drawn = base * np.exp(spread * noise) if base else spread * noise
        out[name] = jnp.asarray(drawn.astype(out[name].dtype))
    for name, factor in factors.items():
        out[name] = (out[name] * factor).astype(out[name].dtype)
    return out
```

```python
import concourse.bass as bass
from concourse import mybir
from contextlib import ExitStack

F32 = mybir.dt.float32
F16 = mybir.dt.float16
I32 = mybir.dt.int32
ALU = mybir.AluOpType
ACT = mybir.ActivationFunctionType
AX = mybir.AxisListType
DVE_ONLY = [mybir.EngineType.DVE]

P = 128
N = 2500
E = 80000
D = 512
KD = D // P
DH = 256
KH = DH // P
R = 8
TILES = -(-N // P)
NP = TILES * P
LAST = N - (TILES - 1) * P
COLS = E // P

GROUP = 5
GROUPS = 5
SCATTER_LOOPS = COLS // (GROUP * GROUPS)

HALF = 6
BODY = 2 * HALF
MOST = (E + TILES * (P - 1)) // P
LOOPS = -(-MOST // BODY)
CH = LOOPS * BODY

BANKS = 4
BATCH = 4
BATCHES = TILES // BATCH
EPS_LN = 1e-5
EPS_NORM = 1e-12
TINY = 2.0 ** -116



class Pass:

    def __init__(self, n, lst, w, row, table, width, dest, off, degree, ready, idx, got, hot, raw, prod, added, dcol):
        self.n, self.lst, self.w, self.row, self.table, self.width = n, lst, w, row, table, width
        self.dest, self.off, self.degree = dest, off, degree
        self.ready, self.idx, self.got, self.hot, self.raw = ready, idx, got, hot, raw
        self.prod, self.added, self.dcol = prod, added, dcol


def build(nc, x, xT, src, dst, rel, ew, wselfT, bself, wrelT, brel, w1, b1, w2, b2, out):
    ctx = ExitStack()
    with ctx:
        def sb(name, shape, dt=F32):
            return ctx.enter_context(nc.sbuf_tensor(name, shape, dt))

        def sem(name):
            return ctx.enter_context(nc.semaphore(name))

        tableH = nc.dram_tensor("tableH", [2 * R * NP, D], F32)
        tableC1 = nc.dram_tensor("tableC1", [NP, DH], F32)
        tableC2 = nc.dram_tensor("tableC2", [NP, DH], F32)
        WORDS = (4, 2)
        sorted_dram = [nc.dram_tensor(f"sorted{d}", [P * CH, WORDS[d]], F32) for d in range(2)]

        region_acc = sb("region_acc", [P, 12500])
        onehotT = region_acc[:, 0:6250].bitcast(F16).rearrange("p (t j) -> p t j", t=TILES)
        runcount = region_acc[:, 6250:12500].bitcast(F16).rearrange("p (t j) -> p t j", t=TILES)
        acc = region_acc[:, 0:TILES * D]
        region_x = sb("region_x", [P, KD * NP])
        xTs = region_x[:, :].rearrange("p (k n) -> p k n", k=KD)
        y = region_x[:, 0:TILES * D].rearrange("p (t f) -> p t f", t=TILES)
        region_w = sb("region_w", [P, 2 * KD * D])
        wbuf = region_w[:, :].rearrange("p (b k o) -> p b k o", b=2, k=KD)
        w1s = region_w[:, 0:KD * DH].rearrange("p (k o) -> p k o", k=KD)
        w2s = region_w[:, KD * DH:2 * KD * DH].rearrange("p (k o) -> p k o", k=KH)
        xt1 = region_w[:, 2 * KD * DH:2 * KD * DH + 2 * D].rearrange("p (b f) -> p b f", b=2)
        b1s = region_w[:, 2 * KD * DH + 2 * D:2 * KD * DH + 2 * D + DH]
        b2s = region_w[:, 2 * KD * DH + 2 * D + DH:2 * KD * DH + 3 * D + DH]
        region_s = sb("region_s", [P, 2 * BATCH * D])
        stage = region_s[:, :].rearrange("p (b t o) -> p b t o", b=2, t=BATCH)
        xrow = region_s[:, 0:4 * D].rearrange("p (b f) -> p b f", b=4)
        edges = sb("edges", [P, 4 * COLS])
        src_i = edges[:, 0:COLS].bitcast(I32)
        dst_i = edges[:, COLS:2 * COLS].bitcast(I32)
        rel_i = edges[:, 2 * COLS:3 * COLS].bitcast(I32)
        ew_f = edges[:, 3 * COLS:4 * COLS]
        list1 = edges[:, 0:2 * CH].rearrange("p (c w) -> p c w", w=2)
        scratch = sb("scratch", [P, 3, CH])
        tmp_i = scratch[:, 0:2, 0:COLS].bitcast(I32)
        posf = scratch[:, 2, 0:COLS]
        degwork = scratch[:, 0, :]
        degpart = scratch[:, 2, :]
        region_r = sb("region_r", [P, TILES * DH])
        rec = [region_r[:, 0:4 * COLS].rearrange("p (j w) -> p j w", w=4),
               region_r[:, 4 * COLS:6 * COLS].rearrange("p (j w) -> p j w", w=2)]
        place = [region_r[:, (6 + d) * COLS:(7 + d) * COLS].bitcast(I32) for d in range(2)]
        acc2 = region_r[:, :]
        place_st = sb("place_st", [P, GROUPS, GROUP], I32)
        rec_st = sb("rec_st", [P, GROUPS, GROUP, 4])
        list0 = sb("list0", [P, CH, 4])
        row_h = [sb("row_h0", [P, CH], I32)[:, :], edges[:, 2 * CH:3 * CH].bitcast(I32)]
        row_s = sb("row_s", [P, CH], I32)
        idx_ring = sb("idx_ring", [P, 2, HALF], I32)
        gathered = sb("gathered", [P, HALF, D])
        onehot = sb("onehot", [P, 2, HALF, P])
        bias = sb("bias", [P, 2, D])
        ident = sb("ident", [P, P])
        before = sb("before", [P, P])
        ones = sb("ones", [P, P])
        lane = sb("lane", [P, P])
        tile_no = sb("tile_no", [P, TILES], F16)
        chunk_no = sb("chunk_no", [P, CH])
        degmask = sb("degmask", [P, CH])
        chunk_tile = [degmask[:, :], scratch[:, 0, :]]
        offsets = sb("offsets", [P, CH], I32)
        off512 = [offsets[0:1, :], offsets[32:33, :]]
        off256 = offsets[64:65, :]
        cnt = sb("cnt", [P, 8, TILES])
        cnt_i = sb("cnt_i", [P, TILES], I32)
        deg = sb("deg", [P, 4, TILES])
        dinv = deg[:, 3, :]
        stats = sb("stats", [P, TILES, 6])
        mv = sb("mv", [P, TILES, 2])
        rstd = sb("rstd", [P, 2, TILES])
        epsc = sb("epsc", [P, 1])

        psum = [ctx.enter_context(nc.psum_tensor(f"ps{i}", [P, 512], F32)) for i in range(8)]
        ps_deg, ps_cnt = psum[6], psum[7]

        s_edges = sem("s_edges")
        s_xT = sem("s_xT")
        s_w = [sem(f"s_w{b}") for b in range(2)]
        s_const = sem("s_const")
        s_const2 = sem("s_const2")
        s_pad = sem("s_pad")
        s_padded = sem("s_padded")
        s_d = sem("s_d")
        s_cnt = sem("s_cnt")
        s_tot = sem("s_tot")
        s_place = sem("s_place")
        s_staged0 = sem("s_staged0")
        s_dx = sem("s_dx")
        s_staged = sem("s_staged")
        s_scat = [sem(f"s_scat{g}") for g in range(GROUPS)]
        s_list = [sem(f"s_list{d}") for d in range(2)]
        s_hmm = sem("s_hmm")
        s_hev = sem("s_hev")
        s_hst = [sem(f"s_hst{b}") for b in range(2)]
        s_tab1 = sem("s_tab1")
        s_tab2 = sem("s_tab2")
        s_b12 = sem("s_b12")
        s_x = [sem(f"s_xrow{b}") for b in range(4)]
        s_res = sem("s_res")
        s_bn = sem("s_bn")
        s_mv = sem("s_mv")
        s_sd = sem("s_sd")
        s_rs = sem("s_rs")
        s_x1 = sem("s_x1")
        s_tp = sem("s_tp")
        s_tpc = sem("s_tpc")
        s_c1 = sem("s_c1")
        s_hs = sem("s_hs")
        s_z = sem("s_z")
        s_zz = sem("s_zz")
        s_dv = sem("s_dv")
        s_sq = sem("s_sq")
        s_out = sem("s_out")
        s_yv = sem("s_yv")

        s_ready = [sem(f"s_ready{d}") for d in range(2)]
        passes = []
        for n, (lst, w, row, table, width, dest, off, degree) in enumerate([
                (list0, None, row_h[0], tableH, D, acc, off512[0], True),
                (list1, None, row_h[1], tableH, D, acc, off512[1], False),
                (list0, list0, row_s, tableC1, DH, acc2, off256, False),
                (list0, list0, row_s, tableC2, DH, acc2, off256, False)]):
            passes.append(Pass(
                n=n, lst=lst, w=w, row=row, table=table, width=width, dest=dest, off=off, degree=degree,
                ready=s_ready[1 if n == 1 else 0],
                idx=sem(f"p{n}_idx"),
                got=[sem(f"p{n}_got{k}") for k in range(HALF)],
                hot=sem(f"p{n}_hot"),
                raw=sem(f"p{n}_raw"),
                prod=sem(f"p{n}_prod"),
                added=sem(f"p{n}_added"),
                dcol=sem(f"p{n}_dcol")))

        block = ctx.enter_context(nc.Block())

        def loop(eng, count, body):
            body(0)
            with eng.Fori(1, count) as i:
                body(i)

        def in_register(eng, value):
            return value if isinstance(value, int) else eng.to_reg(value)

        def later(i):
            return not (isinstance(i, int) and i == 0)

        @block.sync
        def _(sp):
            for a, v in ((src_i, src), (dst_i, dst), (rel_i, rel), (ew_f, ew)):
                sp.dma_start(a, v.rearrange("(p j) -> p j", p=P)).then_inc(s_edges, 16)
            sp.dma_start(xTs[:, :, 0:N], xT.rearrange("(k p) n -> p k n", p=P)).then_inc(s_xT, 16)
            sp.dma_start(wbuf[:, 0], wselfT.rearrange("(k p) o -> p k o", p=P)).then_inc(s_w[0], 16)
            sp.dma_start(bias[:, 0], bself[None, :].partition_broadcast(P)).then_inc(s_w[0], 16)
            wrel_v = wrelT.rearrange("r (k p) o -> r p k o", p=P)

            def load_w(slot, buf):
                sp.dma_start(wbuf[:, buf], wrel_v[bass.ds(slot, 1)].rearrange("a p k o -> p (a k) o")).then_inc(s_w[buf], 16)
                sp.dma_start(bias[:, buf], brel[bass.ds(slot, 1), :].partition_broadcast(P)).then_inc(s_w[buf], 16)

            load_w(0, 1)
            sp.wait_ge(s_pad, 2)
            sp.dma_start(sorted_dram[0].rearrange("(p c) w -> p (c w)", p=P),
                         list0[:, :, :].rearrange("p c w -> p (c w)")).then_inc(s_padded, 16)
            sp.dma_start(sorted_dram[1].rearrange("(p c) w -> p (c w)", p=P),
                         region_s[:, 0:2 * CH]).then_inc(s_padded, 16)
            sp.wait_ge(s_hev, TILES)
            load_w(1, 0)
            table_v = tableH.rearrange("(s b t p) o -> s b p t o", s=2 * R, b=BATCHES, t=BATCH)

            def body(i):
                for h in range(2):
                    for b in range(BATCHES):
                        m = TILES + (i * 2 + h) * TILES + (b + 1) * BATCH
                        st = (h * BATCHES + b) % 2
                        sp.wait_ge(s_hev, m)
                        sp.dma_start(table_v[bass.ds(i * 2 + h, 1), b].rearrange("a p t o -> p (a t) o"),
                                     stage[:, st]).then_inc(s_hst[st], 16)
                    if isinstance(i, int) and i == R - 1:
                        continue
                    load_w(i * 2 + h + 2, 1 - h)

            body(0)
            with sp.Fori(1, R - 1) as i:
                body(i)
            body(R - 1)
            sp.wait_ge(s_hmm, (2 * R + 1) * TILES)
            for b in range(2):
                sp.wait_ge(s_hst[b], 16 * R * BATCHES)
            sp.dma_start(w1s, w1.rearrange("(k p) o -> p k o", p=P)).then_inc(s_b12, 16)
            sp.dma_start(w2s, w2.rearrange("(k p) o -> p k o", p=P)).then_inc(s_b12, 16)
            sp.dma_start(b1s, b1[None, :].partition_broadcast(P)).then_inc(s_b12, 16)
            sp.dma_start(b2s, b2[None, :].partition_broadcast(P)).then_inc(s_b12, 16)
            for t in range(TILES):
                m = P if t < TILES - 1 else LAST
                if t >= 4:
                    sp.wait_ge(s_res, t - 3)
                if t == TILES - 1:
                    sp.wait_ge(s_yv, 1)
                sp.dma_start(xrow[0:m, t % 4], x[t * P:t * P + m, :]).then_inc(s_x[t % 4], 16)
            for t in range(TILES):
                sp.wait_ge(s_hs, t + 1)
                sp.dma_start(tableC1[t * P:(t + 1) * P, :], acc2[:, t * DH:(t + 1) * DH]).then_inc(s_tab1, 16)
            for t in range(TILES):
                sp.wait_ge(s_zz, t + 1)
                sp.dma_start(tableC2[t * P:(t + 1) * P, :], acc2[:, t * DH:(t + 1) * DH]).then_inc(s_tab2, 16)
            for t in range(TILES):
                m = P if t < TILES - 1 else LAST
                sp.wait_ge(s_x1, TILES + t + 1)
                sp.dma_start(out[t * P:t * P + m, :], acc[0:m, t * D:(t + 1) * D]).then_inc(s_out, 16)
            sp.wait_ge(s_out, 16 * TILES)

        @block.gpsimd
        def _(pool):
            nc.gpsimd.memset(ident[:, :], 0.0).then_inc(s_const2, 1)
            nc.gpsimd.memset(before[:, :], 1.0).then_inc(s_const2, 1)
            pool.wait_ge(s_const2, 2)
            nc.gpsimd.affine_select(out=ident[:, :], in_=ident[:, :], compare_op=ALU.not_equal, fill=1.0,
                                    base=0, pattern=[[-1, P]], channel_multiplier=1).then_inc(s_const, 1)
            nc.gpsimd.affine_select(out=before[:, :], in_=before[:, :], compare_op=ALU.is_gt, fill=0.0,
                                    base=0, pattern=[[1, P]], channel_multiplier=-1).then_inc(s_const, 1)
            nc.gpsimd.memset(ones[:, :], 1.0).then_inc(s_const, 1)
            nc.gpsimd.iota(lane[:, :], [[1, P]], base=0, channel_multiplier=0,
                           allow_small_or_imprecise_dtypes=True).then_inc(s_const, 1)
            nc.gpsimd.iota(tile_no[:, :], [[1, TILES]], base=0, channel_multiplier=0,
                           allow_small_or_imprecise_dtypes=True).then_inc(s_const, 1)
            nc.gpsimd.iota(chunk_no[:, :], [[1, CH]], base=0, channel_multiplier=0,
                           allow_small_or_imprecise_dtypes=True).then_inc(s_const, 1)
            pool.wait_ge(s_padded, 32)
            for d in range(2):
                def body(i):
                    for g in range(GROUPS):
                        staged = in_register(pool, (d * SCATTER_LOOPS + i) * GROUPS + g + 1)
                        pool.wait_ge(s_padded, 32)
                        pool.wait_ge(s_staged, staged)
                        for k in range(GROUP):
                            pool.indirect_dma_start(
                                sorted_dram[d][:, :],
                                bass.IndirectOffsetOnAxis(ap=place_st[:, g, k:k + 1], axis=0),
                                rec_st[:, g, k, 0:WORDS[d]], None).then_inc(s_scat[g], 16)
                loop(pool, SCATTER_LOOPS, body)

            for ps in passes:
                if ps.n:
                    pool.wait_ge(passes[ps.n - 1].prod, CH)
                if ps.n == 0:
                    for b in range(2):
                        pool.wait_ge(s_hst[b], 16 * R * BATCHES)
                if ps.n == 2:
                    pool.wait_ge(s_tab1, 16 * TILES)
                if ps.n == 3:
                    pool.wait_ge(s_tab2, 16 * TILES)

                def body(i, ps=ps):
                    for h in range(2):
                        half = in_register(pool, i * 2 + h + 1)
                        pool.wait_ge(ps.ready, 1)
                        pool.wait_ge(ps.idx, half)
                        for k in range(HALF):
                            if later(i) or h:
                                done = in_register(pool, i * BODY + (h - 1) * HALF + k + 1)
                                pool.wait_ge(ps.ready, 1)
                                pool.wait_ge(ps.prod, done)
                            pool.indirect_dma_start(
                                gathered[:, k, 0:ps.width], None, ps.table[:, :],
                                bass.IndirectOffsetOnAxis(ap=idx_ring[:, h, k:k + 1], axis=0)).then_inc(ps.got[k], 16)
                loop(pool, LOOPS, body)

        @block.scalar
        def _(act):
            for d in range(2):
                act.wait_ge(s_place, d + 1)

                def body(i):
                    for g in range(GROUPS):
                        if later(i) or d:
                            act.wait_ge(s_scat[g], 16 * GROUP * (d * SCATTER_LOOPS + i))
                        col = (i * GROUPS + g) * GROUP
                        nc.scalar.copy(place_st[:, g, :], place[d][:, bass.ds(col, GROUP)]).then_inc(s_staged0, 1)
                        nc.scalar.copy(rec_st[:, g, :, 0:WORDS[d]], rec[d][:, bass.ds(col, GROUP), :]).then_inc(s_staged0, 1)
                        act.wait_ge(s_staged0, 2 * ((d * SCATTER_LOOPS + i) * GROUPS + g + 1))
                        act.sem_inc(s_staged, 1)
                loop(act, SCATTER_LOOPS, body)
                for g in range(GROUPS):
                    act.wait_ge(s_scat[g], 16 * GROUP * SCATTER_LOOPS * (d + 1))
                lst = (list0[:, :, :], list1)[d]
                act.dma_start(lst.rearrange("p c w -> p (c w)"),
                              sorted_dram[d].rearrange("(p c) w -> p (c w)", p=P)).then_inc(s_list[d], 16)

            def run_pass(ps):
                act.wait_ge(ps.ready, 1)
                if ps.n:
                    for k in range(HALF):
                        act.wait_ge(passes[ps.n - 1].got[k], 16 * 2 * LOOPS)

                def stage_idx(i, h):
                    if later(i):
                        for k in range(HALF):
                            act.wait_ge(ps.got[k], 16 * (i * 2 + h - 1))
                    nc.scalar.copy(idx_ring[:, h, :], ps.row[:, bass.ds(i * BODY + h * HALF, HALF)]).then_inc(ps.idx, 1)

                def body(i):
                    for h in range(2):
                        stage_idx(i, h)
                        if ps.degree:
                            act.wait_ge(ps.prod, i * BODY + (h + 1) * HALF)
                            nc.scalar.copy(degpart[:, bass.ds(i * BODY + h * HALF, HALF)],
                                           ps_deg[:, h * HALF:(h + 1) * HALF]).then_inc(ps.dcol, 1)
                loop(act, LOOPS, body)

            def transposes(t, blocks, base):
                act.wait_ge(s_tp, base + t + 1)
                if t >= 2 or base:
                    act.wait_ge(s_c1, base + t - 1)
                nc.scalar.copy(xt1[:, t % 2, 0:blocks * P], psum[t % 2][:, 0:blocks * P]).then_inc(s_tpc, 1)

            run_pass(passes[0])
            run_pass(passes[1])
            act.wait_ge(s_mv, TILES)
            act.wait_ge(s_dv, 1)
            nc.scalar.activation(rstd[:, 0, :], mv[:, :, 1], ACT.Sqrt, bias=epsc[:, 0:1]).then_inc(s_sd, 1)
            nc.scalar.activation(deg[:, 2, :], deg[:, 1, :], ACT.Sqrt).then_inc(s_sd, 1)
            for t in range(TILES):
                transposes(t, KD, 0)
            run_pass(passes[2])
            run_pass(passes[3])
            for t in range(TILES):
                transposes(t, KH, TILES)
                act.wait_ge(s_yv, 2 + t)
                nc.scalar.activation(gathered[:, t % 2, :], y[:, t, :], ACT.Square,
                                     accum_out=cnt[:, 0, t:t + 1]).then_inc(s_sq, 1)
            act.wait_ge(s_sq, TILES + 1)
            nc.scalar.activation(cnt[:, 2, :], cnt[:, 1, :], ACT.Sqrt).then_inc(s_sq, 1)
            act.wait_ge(s_mv, 2 * TILES)
            nc.scalar.activation(rstd[:, 0, :], mv[:, :, 1], ACT.Sqrt, bias=epsc[:, 0:1]).then_inc(s_sd, 1)

        @block.vector
        def _(dve):
            steps = [0]

            def link(ins):
                steps[0] += 1
                ins.then_inc(s_d, 1)
                dve.wait_ge(s_d, steps[0])

            link(nc.vector.memset(epsc[:, :], EPS_LN))
            link(nc.vector.memset(list0[:, :, :], 0.0))
            nc.vector.memset(list0[:, :, 0:1], -1.0).then_inc(s_pad, 1)
            link(nc.vector.memset(region_s[:, 0:2 * CH], 0.0))
            nc.vector.memset(region_s[:, 0:2 * CH].rearrange("p (c w) -> p c w", w=2)[:, :, 0:1], -1.0).then_inc(s_pad, 1)
            nc.vector.memset(xTs[:, :, N:NP], 0.0).then_inc(s_dx, 1)
            dve.wait_ge(s_edges, 64)
            dve.wait_ge(s_const, 6)
            for d in range(2):
                key = (dst_i, src_i)[d]
                other = (src_i, dst_i)[d]
                link(nc.vector.tensor_scalar(tmp_i[:, 0, :], key, P - 1, None, ALU.bitwise_and))
                link(nc.vector.tensor_copy(rec[d][:, :, 0], tmp_i[:, 0, :]))
                link(nc.vector.tensor_scalar(rec[d][:, :, 1], rel_i, float(NP), float(d * R * NP), ALU.mult, ALU.add))
                link(nc.vector.tensor_tensor(rec[d][:, :, 1], rec[d][:, :, 1], other, ALU.add))
                if d == 0:
                    link(nc.vector.tensor_copy(rec[0][:, :, 2], ew_f))
                    link(nc.vector.tensor_copy(rec[0][:, :, 3], src_i))
                link(nc.vector.tensor_scalar(tmp_i[:, 1, :], key, 7, None, ALU.logical_shift_right))
                link(nc.vector.tensor_tensor(onehotT, tile_no[:, :].unsqueeze(2).to_broadcast([P, TILES, COLS]),
                                             tmp_i[:, 1:2, :].to_broadcast([P, TILES, COLS]), ALU.is_equal))
                flat = onehotT.rearrange("p t j -> p (t j)")
                link(nc.vector.tensor_tensor_scan(runcount.rearrange("p t j -> p (t j)"), flat, flat, 0.0,
                                                  ALU.add, ALU.max))
                start = cnt[:, 1, :]
                link(nc.vector.memset(start, 0.0))
                link(nc.vector.tensor_copy(cnt[:, 1, 1:TILES], runcount[:, 0:TILES - 1, COLS - 1]))
                nc.vector.tensor_tensor(cnt[:, 0, :], runcount[:, :, COLS - 1], start, ALU.subtract).then_inc(s_cnt, 1)
                dve.wait_ge(s_cnt, d + 1)
                link(nc.vector.tensor_tensor(runcount, runcount, onehotT, ALU.mult))
                link(nc.vector.tensor_reduce(posf, runcount.rearrange("p t j -> p j t"), AX.X, ALU.add))
                dve.wait_ge(s_tot, d + 1)
                link(nc.vector.tensor_scalar(cnt_i[:, :], ps_cnt[:, 32:32 + TILES], float(P - 1), None, ALU.add))
                link(nc.vector.tensor_scalar(cnt_i[:, :], cnt_i[:, :], 7, None, ALU.logical_shift_right))
                link(nc.vector.tensor_copy(cnt[:, 2, :], cnt_i[:, :]))
                link(nc.vector.tensor_tensor_scan(cnt[:, 3, :], cnt[:, 2, :], cnt[:, 2, :], 0.0, ALU.add, ALU.max))
                link(nc.vector.tensor_tensor(cnt[:, 4, :], cnt[:, 3, :], cnt[:, 2, :], ALU.subtract))
                link(nc.vector.scalar_tensor_tensor(out=cnt[:, 5, :], in0=cnt[:, 4, :], scalar=float(P),
                                                    in1=ps_cnt[:, 0:TILES], op0=ALU.mult, op1=ALU.add))
                link(nc.vector.scalar_tensor_tensor(out=cnt[:, 6, :], in0=cnt[:, 5, :], scalar=-1.0,
                                                    in1=start, op0=ALU.add, op1=ALU.subtract))
                for t in range(TILES):
                    link(nc.vector.scalar_tensor_tensor(out=posf, in0=onehotT[:, t, :], scalar=cnt[:, 6, t:t + 1],
                                                        in1=posf, op0=ALU.mult, op1=ALU.add))
                link(nc.vector.tensor_copy(place[d], posf))
                link(nc.vector.tensor_scalar(tmp_i[:, 0, :], place[d], P - 1, None, ALU.bitwise_and))
                link(nc.vector.tensor_scalar(tmp_i[:, 1, :], place[d], 7, None, ALU.logical_shift_right))
                nc.vector.scalar_tensor_tensor(out=place[d], in0=tmp_i[:, 0, :], scalar=float(CH),
                                               in1=tmp_i[:, 1, :], op0=ALU.mult, op1=ALU.add).then_inc(s_place, 1)
                dve.wait_ge(s_place, d + 1)
                link(nc.vector.tensor_scalar(chunk_tile[d], chunk_no[:, :], cnt[:, 3, 0:1], None, ALU.is_ge))
                for t in range(1, TILES - 1):
                    link(nc.vector.scalar_tensor_tensor(out=chunk_tile[d], in0=chunk_no[:, :],
                                                        scalar=cnt[:, 3, t:t + 1], in1=chunk_tile[d],
                                                        op0=ALU.is_ge, op1=ALU.add))
                row = 32 * d
                link(nc.vector.tensor_scalar(off512[d], chunk_tile[d][row:row + 1, :], float(D), None, ALU.mult))
                if d == 0:
                    link(nc.vector.tensor_scalar(off256, chunk_tile[d][64:65, :], float(DH), None, ALU.mult))

            dve.wait_ge(s_w[0], 32)
            for t in range(TILES):
                dve.wait_ge(s_hmm, t + 1)
                nc.vector.tensor_tensor(acc[:, t * D:(t + 1) * D], psum[t % BANKS][:, :], bias[:, 0], ALU.add).then_inc(s_hev, 1)

            def body(i):
                for h in range(2):
                    dve.wait_ge(s_w[1 - h], 32 * (i + 1 + h))
                    for t in range(TILES):
                        m = TILES + (i * 2 + h) * TILES + t
                        bank = (h * TILES + t) % BANKS
                        b = (h * BATCHES + t // BATCH)
                        dve.wait_ge(s_hmm, m + 1)
                        if t % BATCH == 0 and (later(i) or b >= 2):
                            dve.wait_ge(s_hst[b % 2], 16 * (i * BATCHES + b // 2))
                        nc.vector.tensor_tensor(stage[:, b % 2, t % BATCH, :], psum[bank][:, :], bias[:, 1 - h],
                                                ALU.add).then_inc(s_hev, 1)
            dve.wait_ge(s_padded, 32)
            loop(dve, R, body)

            dve.wait_ge(s_list[0], 16)
            nc.vector.tensor_copy(row_s[:, :], list0[:, :, 3])
            nc.vector.tensor_copy(row_h[0], list0[:, :, 1]).then_inc(passes[0].ready, 1)
            dve.wait_ge(s_list[1], 16)
            nc.vector.tensor_copy(row_h[1], list1[:, :, 1]).then_inc(passes[1].ready, 1)

            def run_pass(ps):
                def hots(i, h):
                    lo = i * BODY + h * HALF
                    which = (ps.lst[:, bass.ds(lo, HALF), 0:1]).to_broadcast([P, HALF, P])
                    lanes = lane[:, :].unsqueeze(1).to_broadcast([P, HALF, P])
                    if later(i):
                        dve.wait_ge(ps.prod, i * BODY + (h - 1) * HALF)
                    if ps.w is None:
                        nc.vector.tensor_tensor(onehot[:, h], lanes, which, ALU.is_equal).then_inc(ps.hot, 1)
                    else:
                        nc.vector.tensor_tensor(onehot[:, h], lanes, which, ALU.is_equal).then_inc(ps.raw, 1)
                        dve.wait_ge(ps.raw, i * 2 + h + 1)
                        weight = ps.w[:, bass.ds(lo, HALF), 2:3].to_broadcast([P, HALF, P])
                        nc.vector.tensor_tensor(onehot[:, h], onehot[:, h], weight, ALU.mult).then_inc(ps.hot, 1)

                def adds(i, h):
                    lo = i * BODY + h * HALF
                    _, offs = nc.values_load_multi_w_load_instructions(
                        ps.off[:, bass.ds(lo, HALF)], DVE_ONLY, min_val=0, max_val=(TILES - 1) * ps.width,
                        skip_runtime_bounds_check_because="a chunk's tile is a count of at most TILES - 1 comparisons")
                    for k in range(HALF):
                        dest = ps.dest[:, bass.ds(offs[k], ps.width)]
                        dve.wait_ge(ps.prod, lo + k + 1)
                        if later(i) or h or k:
                            dve.wait_ge(ps.added, lo + k)
                        nc.vector.tensor_tensor(dest, psum[k][:, 0:ps.width], dest, ALU.add).then_inc(ps.added, 1)

                def body(i):
                    hots(i, 0)
                    if later(i):
                        adds(i - 1, 1)
                    hots(i, 1)
                    adds(i, 0)
                loop(dve, LOOPS, body)
                adds(LOOPS - 1, 1)
                dve.wait_ge(ps.added, CH)

            run_pass(passes[0])
            run_pass(passes[1])

            dve.wait_ge(passes[0].dcol, 2 * LOOPS)
            for t in range(TILES):
                link(nc.vector.scalar_tensor_tensor(out=degwork, in0=degmask[:, :], scalar=float(t),
                                                    in1=degpart, op0=ALU.is_equal, op1=ALU.mult))
                link(nc.vector.tensor_reduce(deg[:, 0, t:t + 1], degwork, AX.X, ALU.add))
            link(nc.vector.tensor_scalar(deg[:, 0, :], deg[:, 0, :], 1.0, None, ALU.add))
            nc.vector.tensor_scalar(deg[:, 1, :], deg[:, 0, :], TINY, None, ALU.max).then_inc(s_dv, 1)

            def norm(t0, ready):
                for t in range(TILES):
                    dve.wait_ge(s_res, t0 + t + 1)
                    nc.vector.bn_stats(stats[:, t, :], acc[:, t * D:(t + 1) * D]).then_inc(s_bn, 1)
                for t in range(TILES):
                    dve.wait_ge(s_bn, t0 + t + 1)
                    nc.vector.bn_aggr(mv[:, t, :], stats[:, t, :]).then_inc(s_mv, 1)
                dve.wait_ge(s_sd, ready)
                nc.vector.reciprocal(rstd[:, 1, :], rstd[:, 0, :]).then_inc(s_rs, 1)
                dve.wait_ge(s_rs, 1 if t0 == 0 else 2)
                for t in range(TILES):
                    nc.vector.tensor_scalar(acc[:, t * D:(t + 1) * D], acc[:, t * D:(t + 1) * D], mv[:, t, 0:1],
                                            rstd[:, 1, t:t + 1], ALU.subtract, ALU.mult).then_inc(s_x1, 1)

            for t in range(TILES):
                if t == TILES - 1:
                    dve.wait_ge(s_res, t - 3)
                    nc.vector.memset(xrow[64:P, t % 4], 0.0).then_inc(s_yv, 1)
                dve.wait_ge(s_x[t % 4], 16 * (t // 4 + 1))
                a = acc[:, t * D:(t + 1) * D]
                nc.vector.scalar_tensor_tensor(out=a, in0=a, scalar=0.0, in1=xrow[:, t % 4],
                                               op0=ALU.max, op1=ALU.add).then_inc(s_res, 1)
            norm(0, 2)
            link(nc.vector.reciprocal(deg[:, 1, :], deg[:, 2, :]))
            link(nc.vector.scalar_tensor_tensor(out=dinv, in0=deg[:, 0, :], scalar=0.0, in1=deg[:, 1, :],
                                                op0=ALU.is_gt, op1=ALU.mult))
            for t in range(TILES):
                dve.wait_ge(s_c1, t + 1)
                nc.vector.tensor_scalar(acc2[:, t * DH:(t + 1) * DH], psum[2 + t % 2][:, 0:DH], dinv[:, t:t + 1],
                                        None, ALU.mult).then_inc(s_hs, 1)
            dve.wait_ge(s_tab1, 16 * TILES)
            run_pass(passes[2])
            for t in range(TILES):
                a = acc2[:, t * DH:(t + 1) * DH]
                nc.vector.scalar_tensor_tensor(out=a, in0=a, scalar=dinv[:, t:t + 1], in1=b1s,
                                               op0=ALU.mult, op1=ALU.add).then_inc(s_z, 1)
            for t in range(TILES):
                a = acc2[:, t * DH:(t + 1) * DH]
                dve.wait_ge(s_z, t + 1)
                nc.vector.tensor_scalar(a, a, 0.0, dinv[:, t:t + 1], ALU.max, ALU.mult).then_inc(s_zz, 1)
            dve.wait_ge(s_tab2, 16 * TILES)
            run_pass(passes[3])
            dve.wait_ge(s_b12, 64)
            for t in range(TILES):
                dve.wait_ge(s_c1, TILES + t + 1)
                nc.vector.scalar_tensor_tensor(out=y[:, t, :], in0=psum[2 + t % 2][:, :], scalar=dinv[:, t:t + 1],
                                               in1=b2s, op0=ALU.mult, op1=ALU.add).then_inc(s_yv, 1)
            dve.wait_ge(s_sq, TILES)
            nc.vector.tensor_scalar(cnt[:, 1, :], cnt[:, 0, :], TINY, None, ALU.max).then_inc(s_sq, 1)
            dve.wait_ge(s_sq, TILES + 2)
            link(nc.vector.tensor_scalar(cnt[:, 3, :], cnt[:, 2, :], EPS_NORM, None, ALU.max))
            link(nc.vector.reciprocal(cnt[:, 4, :], cnt[:, 3, :]))
            for t in range(TILES):
                a = acc[:, t * D:(t + 1) * D]
                nc.vector.scalar_tensor_tensor(out=a, in0=y[:, t, :], scalar=cnt[:, 4, t:t + 1], in1=a,
                                               op0=ALU.mult, op1=ALU.add).then_inc(s_res, 1)
            norm(TILES, 3)

        @block.tensor
        def _(pe):
            for d in range(2):
                pe.wait_ge(s_cnt, d + 1)
                nc.tensor.matmul(ps_cnt[:, 0:TILES], before[:, :], cnt[:, 0, :], start=True, stop=True)
                nc.tensor.matmul(ps_cnt[:, 32:32 + TILES], ones[:, :], cnt[:, 0, :], start=True, stop=True).then_inc(s_tot, 1)

            pe.wait_ge(s_xT, 16)
            pe.wait_ge(s_dx, 1)
            pe.wait_ge(s_w[0], 32)
            for t in range(TILES):
                if t >= BANKS:
                    pe.wait_ge(s_hev, t - BANKS + 1)
                for k in range(KD):
                    mm = nc.tensor.matmul(psum[t % BANKS][:, :], xTs[:, k, t * P:(t + 1) * P], wbuf[:, 0, k, :],
                                          start=(k == 0), stop=(k == KD - 1))
                mm.then_inc(s_hmm, 1)

            def body(i):
                for h in range(2):
                    pe.wait_ge(s_w[1 - h], 32 * (i + 1 + h))
                    for t in range(TILES):
                        m = TILES + (i * 2 + h) * TILES + t
                        bank = (h * TILES + t) % BANKS
                        pe.wait_ge(s_hev, m - BANKS + 1)
                        for k in range(KD):
                            mm = nc.tensor.matmul(psum[bank][:, :], xTs[:, k, t * P:(t + 1) * P],
                                                  wbuf[:, 1 - h, k, :], start=(k == 0), stop=(k == KD - 1))
                        mm.then_inc(s_hmm, 1)
            loop(pe, R, body)
            pe.wait_ge(s_hev, (2 * R + 1) * TILES)

            def run_pass(ps):
                def body(i):
                    for h in range(2):
                        pe.wait_ge(ps.hot, i * 2 + h + 1)
                        if ps.degree and (later(i)):
                            pe.wait_ge(ps.dcol, i * 2 + h - 1)
                        for k in range(HALF):
                            if later(i) or h:
                                pe.wait_ge(ps.added, i * BODY + (h - 1) * HALF + k + 1)
                            pe.wait_ge(ps.got[k], 16 * (i * 2 + h + 1))
                            if ps.degree:
                                nc.tensor.matmul(ps_deg[:, h * HALF + k:h * HALF + k + 1], onehot[:, h, k, :],
                                                 list0[:, bass.ds(i * BODY + h * HALF + k, 1), 2:3].rearrange("p a b -> p (a b)"),
                                                 start=True, stop=True)
                            nc.tensor.matmul(psum[k][:, 0:ps.width], onehot[:, h, k, :], gathered[:, k, 0:ps.width],
                                             start=True, stop=True).then_inc(ps.prod, 1)
                loop(pe, LOOPS, body)

            run_pass(passes[0])
            run_pass(passes[1])

            def transpose_and_multiply(source, blocks, weight, width, ready, base, column):
                def multiply(t):
                    pe.wait_ge(s_tpc, base + t + 1)
                    if t >= 2:
                        pe.wait_ge(*column(t - 2))
                    for k in range(blocks):
                        mm = nc.tensor.matmul(psum[2 + t % 2][:, 0:width], xt1[:, t % 2, k * P:(k + 1) * P],
                                              weight[:, k, :], start=(k == 0), stop=(k == blocks - 1))
                    mm.then_inc(s_c1, 1)
                for t in range(TILES):
                    if ready is not None:
                        pe.wait_ge(ready, t + 1)
                    if t >= 2:
                        pe.wait_ge(s_tpc, base + t - 1)
                    for k in range(blocks):
                        lo = (t * blocks + k) * P
                        mm = nc.tensor.transpose(psum[t % 2][:, k * P:(k + 1) * P], source[:, lo:lo + P], ident[:, :])
                    mm.then_inc(s_tp, 1)
                    if t:
                        multiply(t - 1)
                multiply(TILES - 1)

            pe.wait_ge(s_b12, 64)
            pe.wait_ge(passes[1].added, CH)
            transpose_and_multiply(acc, KD, w1s, DH, s_x1, 0, lambda t: (s_hs, t + 1))
            run_pass(passes[2])
            run_pass(passes[3])
            pe.wait_ge(passes[3].added, CH)
            transpose_and_multiply(acc2, KH, w2s, D, None, TILES, lambda t: (s_yv, t + 2))


def kernel(**inputs):
    import numpy as _np
    import concourse.bacc as _bacc
    from concourse import mybir as _mybir
    from concourse.bass_utils import run_bass_kernel_spmd as _run

    given = {k: _np.asarray(v) for k, v in inputs.items()}
    laid = [
        ("x", given["x"]), ("xT", given["x"].T),
        ("src", given["src"]), ("dst", given["dst"]), ("rel", given["edge_type_8"]), ("ew", given["edge_weight"]),
        ("wselfT", given["L0_gnn_W_self"].T), ("bself", given["L0_gnn_b_self"]),
        ("wrelT", _np.roll(given["L0_gnn_W_rel"], R, axis=0).transpose(0, 2, 1)),
        ("brel", _np.roll(given["L0_gnn_b_rel"], R, axis=0)),
        ("w1", given["L1_gnn_W1"]), ("b1", given["L1_gnn_b1"]),
        ("w2", given["L1_gnn_W2"]), ("b2", given["L1_gnn_b2"]),
    ]
    nc = _bacc.Bacc("TRN2", target_bir_lowering=False, num_devices=1)
    arrays, args = {}, []
    for name, a in laid:
        a = _np.ascontiguousarray(a)
        arrays[f"in_{name}_dram"] = a
        args.append(nc.dram_tensor(f"in_{name}_dram", a.shape, _mybir.dt.from_np(a.dtype), kind="ExternalInput").ap())
    args.append(nc.dram_tensor("out_0_dram", (N, D), _mybir.dt.float32, kind="ExternalOutput").ap())
    build(nc, *args)
    r = _run(nc, [arrays], core_ids=[0])
    return r.results[0]["out_0_dram"]
```

```python
import concourse.bass as bass
from concourse import mybir
from contextlib import ExitStack

F32 = mybir.dt.float32
F16 = mybir.dt.float16
I32 = mybir.dt.int32
ALU = mybir.AluOpType
ACT = mybir.ActivationFunctionType
AX = mybir.AxisListType
DVE_ONLY = [mybir.EngineType.DVE]

P = 128
N = 2500
E = 80000
D = 512
KD = D // P
DH = 256
KH = DH // P
R = 8
TILES = -(-N // P)
NP = TILES * P
LAST = N - (TILES - 1) * P
COLS = E // P

GROUP = 5
GROUPS = 5
SCATTER_LOOPS = COLS // (GROUP * GROUPS)

SLOTS = 8
HALF = SLOTS // 2
HPAIRS = HALF // 2
PAIR = 2 * P
MOST = (E + TILES * (PAIR - 1)) // PAIR
LOOPS = -(-MOST // (2 * HPAIRS))
HALVES = 2 * LOOPS
PAIRS = LOOPS * 2 * HPAIRS
CH = 2 * PAIRS
AHALF = 2
ACOLS = 2 * HALVES * AHALF
CELLS = NP * NP

BANKS = 4
BATCH = 4
BATCHES = TILES // BATCH
EPS_LN = 1e-5
EPS_NORM = 1e-12
TINY = 2.0 ** -116



class Pass:

    def __init__(self, n, lst, row, off, degree, ready, idx, got, hot, prod, added, dcol):
        self.n, self.lst, self.row, self.off, self.degree = n, lst, row, off, degree
        self.ready, self.idx, self.got, self.hot = ready, idx, got, hot
        self.prod, self.added, self.dcol = prod, added, dcol


def build(nc, x, xT, src, dst, rel, ew, wselfT, bself, wrelT, brel, w1, b1, w2, b2, out):
    ctx = ExitStack()
    with ctx:
        def sb(name, shape, dt=F32):
            return ctx.enter_context(nc.sbuf_tensor(name, shape, dt))

        def sem(name):
            return ctx.enter_context(nc.semaphore(name))

        tableH = nc.dram_tensor("tableH", [2 * R * NP, D], F32)
        matrix = nc.dram_tensor("matrix", [CELLS + P, 1], F32)
        WORDS = (3, 2)
        sorted_dram = [nc.dram_tensor(f"sorted{d}", [P * CH, WORDS[d]], F32) for d in range(2)]

        region_acc = sb("region_acc", [P, 12500])
        onehotT = region_acc[:, 0:6250].bitcast(F16).rearrange("p (t j) -> p t j", t=TILES)
        runcount = region_acc[:, 6250:12500].bitcast(F16).rearrange("p (t j) -> p t j", t=TILES)
        acc = region_acc[:, 0:TILES * D]
        region_x = sb("region_x", [P, KD * NP])
        xTs = region_x[:, :].rearrange("p (k n) -> p k n", k=KD)
        hidden = region_x[:, 2 * NP:4 * NP].rearrange("p (t f) -> p t f", t=TILES)
        y = region_x[:, 0:TILES * D].rearrange("p (t f) -> p t f", t=TILES)
        region_w = sb("region_w", [P, 2 * KD * D])
        wbuf = region_w[:, :].rearrange("p (b k o) -> p b k o", b=2, k=KD)
        w1s = region_w[:, 0:KD * DH].rearrange("p (k o) -> p k o", k=KD)
        w2s = region_w[:, KD * DH:2 * KD * DH].rearrange("p (k o) -> p k o", k=KH)
        xt1 = region_w[:, 2 * KD * DH:2 * KD * DH + 2 * D].rearrange("p (b f) -> p b f", b=2)
        b1s = region_w[:, 2 * KD * DH + 2 * D:2 * KD * DH + 2 * D + DH]
        b2s = region_w[:, 2 * KD * DH + 2 * D + DH:2 * KD * DH + 3 * D + DH]
        region_s = sb("region_s", [P, 2 * BATCH * D])
        stage = region_s[:, :].rearrange("p (b t o) -> p b t o", b=2, t=BATCH)
        xrow = region_s[:, 0:4 * D].rearrange("p (b f) -> p b f", b=4)
        edges = sb("edges", [P, 3 * CH + 8])
        src_i = edges[:, 0:COLS].bitcast(I32)
        dst_i = edges[:, COLS:2 * COLS].bitcast(I32)
        rel_i = edges[:, 2 * COLS:3 * COLS].bitcast(I32)
        list1 = edges[:, 0:2 * CH].rearrange("p (c w) -> p c w", w=2)
        ew_f = sb("ew_f", [P, ACOLS])
        cell = sb("cell", [P, ACOLS])
        scratch = sb("scratch", [P, 3, CH])
        tmp_i = scratch[:, 0:2, 0:COLS].bitcast(I32)
        posf = scratch[:, 2, 0:COLS]
        degwork = scratch[:, 0, 0:PAIRS]
        degpart = scratch[:, 2, 0:PAIRS]
        region_r = sb("region_r", [P, TILES * DH])
        rec = [region_r[:, 0:3 * COLS].rearrange("p (j w) -> p j w", w=3),
               region_r[:, 3 * COLS:5 * COLS].rearrange("p (j w) -> p j w", w=2)]
        place = [region_r[:, (6 + d) * COLS:(7 + d) * COLS].bitcast(I32) for d in range(2)]
        sent = region_r[:, :].rearrange("p (t f) -> p t f", t=TILES)
        place_st = sb("place_st", [P, GROUPS, GROUP], I32)
        rec_st = sb("rec_st", [P, GROUPS, GROUP, 3])
        list0 = sb("list0", [P, CH, 3])
        row_h = [scratch[:, 1, :].bitcast(I32), edges[:, 2 * CH:3 * CH].bitcast(I32)]
        idx_ring = sb("idx_ring", [P, 2, HALF], I32)
        gathered = sb("gathered", [P, SLOTS, D])
        mbuf = [region_x[:, 0:NP], region_x[:, NP:2 * NP],
                gathered[:, :, :].rearrange("p s f -> p (s f)")[:, 0:NP]]
        onehot = sb("onehot", [P, 2, HALF, P])
        bias = sb("bias", [P, 2, D])
        diag = sb("diag", [P, 2, AHALF, P])
        equal = sb("equal", [P, 2, AHALF, P])
        earlier = sb("earlier", [P, 2, AHALF, P], F16)
        rank = sb("rank", [P, 2, AHALF])
        nowhere = sb("nowhere", [P, 1])
        to_nowhere = sb("to_nowhere", [P, 2, AHALF])
        acell = sb("acell", [P, 2, AHALF], I32)
        asum = sb("asum", [P, 2, AHALF])
        ident = sb("ident", [P, P])
        before = sb("before", [P, P])
        after = sb("after", [P, P])
        ones = sb("ones", [P, P])
        lane = sb("lane", [P, P])
        tile_no = sb("tile_no", [P, TILES], F16)
        pair_no = sb("pair_no", [P, PAIRS])
        degmask = sb("degmask", [P, PAIRS])
        pair_tile = [degmask[:, :], scratch[:, 0, 0:PAIRS]]
        offsets = sb("offsets", [P, PAIRS], I32)
        off512 = [offsets[0:1, :], offsets[32:33, :]]
        cnt = sb("cnt", [P, 8, TILES])
        cnt_i = sb("cnt_i", [P, TILES], I32)
        deg = sb("deg", [P, 4, TILES])
        dinv = deg[:, 3, :]
        stats = sb("stats", [P, TILES, 6])
        mv = sb("mv", [P, TILES, 2])
        rstd = sb("rstd", [P, 2, TILES])
        epsc = sb("epsc", [P, 1])

        psum = [ctx.enter_context(nc.psum_tensor(f"ps{i}", [P, 512], F32)) for i in range(8)]
        ps_spread, ps_deg, ps_cnt = (psum[4], psum[7]), (psum[5], psum[6]), psum[7]
        SUMS = AHALF * P

        s_edges = sem("s_edges")
        s_xT = sem("s_xT")
        s_w = [sem(f"s_w{b}") for b in range(2)]
        s_const = sem("s_const")
        s_const2 = sem("s_const2")
        s_pad = sem("s_pad")
        s_padded = sem("s_padded")
        s_d = sem("s_d")
        s_cnt = sem("s_cnt")
        s_tot = sem("s_tot")
        s_place = sem("s_place")
        s_staged0 = sem("s_staged0")
        s_dx = sem("s_dx")
        s_staged = sem("s_staged")
        s_scat = [sem(f"s_scat{g}") for g in range(GROUPS)]
        s_list = [sem(f"s_list{d}") for d in range(2)]
        s_hmm = sem("s_hmm")
        s_hev = sem("s_hev")
        s_hst = [sem(f"s_hst{b}") for b in range(2)]
        s_zero = sem("s_zero")
        s_zeroed = sem("s_zeroed")
        s_cell = sem("s_cell")
        s_diag = sem("s_diag")
        s_spread = sem("s_spread")
        s_equal = sem("s_equal")
        s_rank = sem("s_rank")
        s_nw = sem("s_nw")
        s_acell = sem("s_acell")
        s_sum = sem("s_sum")
        s_asum = sem("s_asum")
        s_added = sem("s_added")
        s_m = [sem(f"s_m{b}") for b in range(3)]
        s_conv = sem("s_conv")
        s_last = sem("s_last")
        s_b12 = sem("s_b12")
        s_x = [sem(f"s_xrow{b}") for b in range(4)]
        s_res = sem("s_res")
        s_bn = sem("s_bn")
        s_mv = sem("s_mv")
        s_sd = sem("s_sd")
        s_rs = sem("s_rs")
        s_x1 = sem("s_x1")
        s_tp = sem("s_tp")
        s_tpc = sem("s_tpc")
        s_c1 = sem("s_c1")
        s_hs = sem("s_hs")
        s_z = sem("s_z")
        s_zz = sem("s_zz")
        s_dv = sem("s_dv")
        s_sq = sem("s_sq")
        s_out = sem("s_out")
        s_yv = sem("s_yv")

        s_ready = [sem(f"s_ready{d}") for d in range(2)]
        passes = []
        for n, (lst, row, off, degree) in enumerate([(list0, row_h[0], off512[0], True),
                                                     (list1, row_h[1], off512[1], False)]):
            passes.append(Pass(
                n=n, lst=lst, row=row, off=off, degree=degree,
                ready=s_ready[n],
                idx=sem(f"p{n}_idx"),
                got=[sem(f"p{n}_got{k}") for k in range(SLOTS)],
                hot=sem(f"p{n}_hot"),
                prod=sem(f"p{n}_prod"),
                added=sem(f"p{n}_added"),
                dcol=sem(f"p{n}_dcol")))

        block = ctx.enter_context(nc.Block())

        def loop(eng, count, body):
            body(0)
            with eng.Fori(1, count - 1) as i:
                body(i)
            body(count - 1)

        def in_register(eng, value):
            return value if isinstance(value, int) else eng.to_reg(value)

        def later(i):
            return not (isinstance(i, int) and i == 0)

        def two_after(i, h):
            return None if isinstance(i, int) and i == LOOPS - 1 else (i + 1, h)

        def after_half(i, h):
            if h == 0:
                return i, 1
            return None if isinstance(i, int) and i == LOOPS - 1 else (i + 1, 0)

        @block.sync
        def _(sp):
            for a, v in ((src_i, src), (dst_i, dst), (rel_i, rel), (ew_f[:, 0:COLS], ew)):
                sp.dma_start(a, v.rearrange("(p j) -> p j", p=P)).then_inc(s_edges, 16)
            sp.dma_start(xTs[:, :, 0:N], xT.rearrange("(k p) n -> p k n", p=P)).then_inc(s_xT, 16)
            sp.dma_start(wbuf[:, 0], wselfT.rearrange("(k p) o -> p k o", p=P)).then_inc(s_w[0], 16)
            sp.dma_start(bias[:, 0], bself[None, :].partition_broadcast(P)).then_inc(s_w[0], 16)
            wrel_v = wrelT.rearrange("r (k p) o -> r p k o", p=P)

            def load_w(slot, buf):
                sp.dma_start(wbuf[:, buf], wrel_v[bass.ds(slot, 1)].rearrange("a p k o -> p (a k) o")).then_inc(s_w[buf], 16)
                sp.dma_start(bias[:, buf], brel[bass.ds(slot, 1), :].partition_broadcast(P)).then_inc(s_w[buf], 16)

            load_w(0, 1)
            sp.wait_ge(s_zero, 1)
            for t in range(TILES):
                sp.dma_start(matrix[t * P * NP:(t + 1) * P * NP, :].rearrange("(p c) w -> p (c w)", p=P),
                             mbuf[2]).then_inc(s_zeroed, 16)
            sp.dma_start(matrix[CELLS:CELLS + P, :], gathered[:, 0, 0:1]).then_inc(s_zeroed, 16)
            sp.wait_ge(s_pad, 2)
            sp.dma_start(sorted_dram[0].rearrange("(p c) w -> p (c w)", p=P),
                         list0[:, :, :].rearrange("p c w -> p (c w)")).then_inc(s_padded, 16)
            sp.dma_start(sorted_dram[1].rearrange("(p c) w -> p (c w)", p=P),
                         region_s[:, 0:2 * CH]).then_inc(s_padded, 16)
            sp.wait_ge(s_hev, TILES)
            load_w(1, 0)
            table_v = tableH.rearrange("(s b t p) o -> s b p t o", s=2 * R, b=BATCHES, t=BATCH)

            def body(i):
                for h in range(2):
                    for b in range(BATCHES):
                        m = TILES + (i * 2 + h) * TILES + (b + 1) * BATCH
                        st = (h * BATCHES + b) % 2
                        sp.wait_ge(s_hev, m)
                        sp.dma_start(table_v[bass.ds(i * 2 + h, 1), b].rearrange("a p t o -> p (a t) o"),
                                     stage[:, st]).then_inc(s_hst[st], 16)
                    if isinstance(i, int) and i == R - 1:
                        continue
                    load_w(i * 2 + h + 2, 1 - h)

            loop(sp, R, body)
            sp.wait_ge(s_hmm, (2 * R + 1) * TILES)
            for b in range(2):
                sp.wait_ge(s_hst[b], 16 * R * BATCHES)
            sp.dma_start(w1s, w1.rearrange("(k p) o -> p k o", p=P)).then_inc(s_b12, 16)
            sp.dma_start(w2s, w2.rearrange("(k p) o -> p k o", p=P)).then_inc(s_b12, 16)
            sp.dma_start(b1s, b1[None, :].partition_broadcast(P)).then_inc(s_b12, 16)
            sp.dma_start(b2s, b2[None, :].partition_broadcast(P)).then_inc(s_b12, 16)
            for t in range(TILES):
                m = P if t < TILES - 1 else LAST
                if t >= 4:
                    sp.wait_ge(s_res, t - 3)
                if t == TILES - 1:
                    sp.wait_ge(s_yv, 1)
                sp.dma_start(xrow[0:m, t % 4], x[t * P:t * P + m, :]).then_inc(s_x[t % 4], 16)
            sp.wait_ge(s_added, 16 * ACOLS)
            sp.wait_ge(passes[1].prod, PAIRS)
            for n in range(2 * TILES):
                t, b = n % TILES, n % 3
                if n >= 3:
                    sp.wait_ge(s_conv, n - 2)
                sp.dma_start(mbuf[b], matrix[t * P * NP:(t + 1) * P * NP, :].rearrange("(p c) w -> p (c w)", p=P)
                             ).then_inc(s_m[b], 16)
            for t in range(TILES):
                m = P if t < TILES - 1 else LAST
                sp.wait_ge(s_x1, TILES + t + 1)
                sp.dma_start(out[t * P:t * P + m, :], acc[0:m, t * D:(t + 1) * D]).then_inc(s_out, 16)
            sp.wait_ge(s_out, 16 * TILES)

        @block.gpsimd
        def _(pool):
            nc.gpsimd.memset(ident[:, :], 0.0).then_inc(s_const2, 1)
            nc.gpsimd.memset(before[:, :], 1.0).then_inc(s_const2, 1)
            pool.wait_ge(s_const2, 2)
            nc.gpsimd.affine_select(out=ident[:, :], in_=ident[:, :], compare_op=ALU.not_equal, fill=1.0,
                                    base=0, pattern=[[-1, P]], channel_multiplier=1).then_inc(s_const, 1)
            nc.gpsimd.memset(after[:, :], 1.0).then_inc(s_const2, 1)
            pool.wait_ge(s_const2, 3)
            nc.gpsimd.affine_select(out=after[:, :], in_=after[:, :], compare_op=ALU.is_gt, fill=0.0,
                                    base=0, pattern=[[-1, P]], channel_multiplier=1).then_inc(s_const, 1)
            nc.gpsimd.iota(nowhere[:, :], [[1, 1]], base=CELLS, channel_multiplier=1,
                           allow_small_or_imprecise_dtypes=True).then_inc(s_const, 1)
            nc.gpsimd.affine_select(out=before[:, :], in_=before[:, :], compare_op=ALU.is_gt, fill=0.0,
                                    base=0, pattern=[[1, P]], channel_multiplier=-1).then_inc(s_const, 1)
            nc.gpsimd.memset(ones[:, :], 1.0).then_inc(s_const, 1)
            nc.gpsimd.iota(lane[:, :], [[1, P]], base=0, channel_multiplier=0,
                           allow_small_or_imprecise_dtypes=True).then_inc(s_const, 1)
            nc.gpsimd.iota(tile_no[:, :], [[1, TILES]], base=0, channel_multiplier=0,
                           allow_small_or_imprecise_dtypes=True).then_inc(s_const, 1)
            nc.gpsimd.iota(pair_no[:, :], [[1, PAIRS]], base=0, channel_multiplier=0,
                           allow_small_or_imprecise_dtypes=True).then_inc(s_const, 1)
            pool.wait_ge(s_padded, 32)
            for d in range(2):
                def body(i):
                    for g in range(GROUPS):
                        staged = in_register(pool, (d * SCATTER_LOOPS + i) * GROUPS + g + 1)
                        pool.wait_ge(s_padded, 32)
                        pool.wait_ge(s_staged, staged)
                        for k in range(GROUP):
                            pool.indirect_dma_start(
                                sorted_dram[d][:, :],
                                bass.IndirectOffsetOnAxis(ap=place_st[:, g, k:k + 1], axis=0),
                                rec_st[:, g, k, 0:WORDS[d]], None).then_inc(s_scat[g], 16)
                loop(pool, SCATTER_LOOPS, body)

            def add_column(turn, h, k):
                number = (turn * 2 + h) * AHALF + k
                cells = in_register(pool, turn * 2 + h + 1)
                before_it = in_register(pool, number * 16)
                pool.wait_ge(s_zeroed, 16 * (TILES + 1))
                pool.wait_ge(s_acell, cells)
                pool.wait_ge(s_asum, cells)
                if not (isinstance(number, int) and number == 0):
                    pool.wait_ge(s_added, before_it)
                pool.indirect_dma_start(
                    matrix[:, :], bass.IndirectOffsetOnAxis(ap=acell[:, h, k:k + 1], axis=0),
                    asum[:, h, k:k + 1], None, compute_op=ALU.add).then_inc(s_added, 16)

            for ps in passes:
                if ps.n:
                    pool.wait_ge(passes[ps.n - 1].prod, PAIRS)
                if ps.n == 0:
                    for b in range(2):
                        pool.wait_ge(s_hst[b], 16 * R * BATCHES)

                def body(i, ps=ps):
                    for h in range(2):
                        half = in_register(pool, i * 2 + h + 1)
                        pool.wait_ge(ps.ready, 1)
                        pool.wait_ge(ps.idx, half)
                        for k in range(HALF):
                            slot = h * HALF + k
                            if later(i) and k % 2 == 0:
                                done = in_register(pool, (i * SLOTS - SLOTS + slot) // 2 + 1 if isinstance(i, int)
                                                   else i * (SLOTS // 2) - SLOTS // 2 + slot // 2 + 1)
                                pool.wait_ge(ps.ready, 1)
                                pool.wait_ge(ps.prod, done)
                            pool.indirect_dma_start(
                                gathered[:, slot, :], None, tableH[:, :],
                                bass.IndirectOffsetOnAxis(ap=idx_ring[:, h, k:k + 1], axis=0)).then_inc(ps.got[slot], 16)
                            if k % 2 and (ps.n or later(i) or h):
                                turn = ps.n * LOOPS + i
                                add_column(turn if h else turn - 1, 1 - h, k // 2)
                loop(pool, LOOPS, body)
            for k in range(AHALF):
                add_column(2 * LOOPS - 1, 1, k)

        @block.scalar
        def _(act):
            for d in range(2):
                act.wait_ge(s_place, d + 1)

                def body(i):
                    for g in range(GROUPS):
                        if later(i) or d:
                            act.wait_ge(s_scat[g], 16 * GROUP * (d * SCATTER_LOOPS + i))
                        col = (i * GROUPS + g) * GROUP
                        nc.scalar.copy(place_st[:, g, :], place[d][:, bass.ds(col, GROUP)]).then_inc(s_staged0, 1)
                        nc.scalar.copy(rec_st[:, g, :, 0:WORDS[d]], rec[d][:, bass.ds(col, GROUP), :]).then_inc(s_staged0, 1)
                        act.wait_ge(s_staged0, 2 * ((d * SCATTER_LOOPS + i) * GROUPS + g + 1))
                        act.sem_inc(s_staged, 1)
                loop(act, SCATTER_LOOPS, body)
                for g in range(GROUPS):
                    act.wait_ge(s_scat[g], 16 * GROUP * SCATTER_LOOPS * (d + 1))
                act.wait_ge(s_cell, 1)
                lst = (list0[:, :, :], list1)[d]
                act.dma_start(lst.rearrange("p c w -> p (c w)"),
                              sorted_dram[d].rearrange("(p c) w -> p (c w)", p=P)).then_inc(s_list[d], 16)

            def run_pass(ps):
                act.wait_ge(ps.ready, 1)
                if ps.n:
                    for k in range(SLOTS):
                        act.wait_ge(passes[ps.n - 1].got[k], 16 * LOOPS)
                first = ps.n * HALVES

                def diagonals(i, h):
                    if later(i) or ps.n:
                        act.wait_ge(s_spread, first + i * 2 + h - 1)
                    for k in range(AHALF):
                        col = (first + i * 2 + h) * AHALF + k
                        nc.scalar.activation(diag[:, h, k, :], ident[:, :], ACT.Copy,
                                             scale=cell[:, bass.ds(col, 1)]).then_inc(s_diag, 1)

                def rows(i, h):
                    if later(i):
                        for k in range(HALF):
                            act.wait_ge(ps.got[h * HALF + k], 16 * i)
                    nc.scalar.copy(idx_ring[:, h, :], ps.row[:, bass.ds(i * SLOTS + h * HALF, HALF)]).then_inc(ps.idx, 1)

                def sums(i, h):
                    act.wait_ge(s_sum, first + i * 2 + h + 1)
                    if later(i) or ps.n:
                        act.wait_ge(s_added, 16 * AHALF * (first + i * 2 + h - 1))
                    nc.scalar.copy(asum[:, h, :], ps_spread[h][:, SUMS:SUMS + AHALF]).then_inc(s_asum, 1)

                def body(i):
                    if not later(i):
                        rows(0, 0)
                        diagonals(0, 0)
                        diagonals(0, 1)
                    for h in range(2):
                        if two_after(i, h):
                            diagonals(*two_after(i, h))
                        if after_half(i, h):
                            rows(*after_half(i, h))
                        sums(i, h)
                        if ps.degree:
                            act.wait_ge(ps.prod, (i * 2 + h + 1) * HPAIRS)
                            nc.scalar.copy(degpart[:, bass.ds((i * 2 + h) * HPAIRS, HPAIRS)],
                                           ps_deg[h][:, 0:HPAIRS]).then_inc(ps.dcol, 1)
                loop(act, LOOPS, body)

            def transposes(t, blocks, base):
                act.wait_ge(s_tp, base + t + 1)
                if t >= 2 or base:
                    act.wait_ge(s_c1, base + t - 1)
                nc.scalar.copy(xt1[:, t % 2, 0:blocks * P], psum[t % 2][:, 0:blocks * P]).then_inc(s_tpc, 1)

            run_pass(passes[0])
            run_pass(passes[1])
            act.wait_ge(s_mv, TILES)
            act.wait_ge(s_dv, 1)
            nc.scalar.activation(rstd[:, 0, :], mv[:, :, 1], ACT.Sqrt, bias=epsc[:, 0:1]).then_inc(s_sd, 1)
            nc.scalar.activation(deg[:, 2, :], deg[:, 1, :], ACT.Sqrt).then_inc(s_sd, 1)
            for t in range(TILES):
                transposes(t, KD, 0)
            for t in range(TILES):
                transposes(t, KH, TILES)
                act.wait_ge(s_yv, 2 + t)
                nc.scalar.activation(gathered[:, t % 2, :], y[:, t, :], ACT.Square,
                                     accum_out=cnt[:, 0, t:t + 1]).then_inc(s_sq, 1)
            act.wait_ge(s_sq, TILES + 1)
            nc.scalar.activation(cnt[:, 2, :], cnt[:, 1, :], ACT.Sqrt).then_inc(s_sq, 1)
            act.wait_ge(s_mv, 2 * TILES)
            nc.scalar.activation(rstd[:, 0, :], mv[:, :, 1], ACT.Sqrt, bias=epsc[:, 0:1]).then_inc(s_sd, 1)

        @block.vector
        def _(dve):
            steps = [0]

            def link(ins):
                steps[0] += 1
                ins.then_inc(s_d, 1)
                dve.wait_ge(s_d, steps[0])

            link(nc.vector.memset(epsc[:, :], EPS_LN))
            link(nc.vector.memset(list0[:, :, :], 0.0))
            nc.vector.memset(list0[:, :, 0:1], -1.0).then_inc(s_pad, 1)
            link(nc.vector.memset(region_s[:, 0:2 * CH], 0.0))
            nc.vector.memset(region_s[:, 0:2 * CH].rearrange("p (c w) -> p c w", w=2)[:, :, 0:1], -1.0).then_inc(s_pad, 1)
            nc.vector.memset(xTs[:, :, N:NP], 0.0).then_inc(s_dx, 1)
            nc.vector.memset(mbuf[2], 0.0).then_inc(s_zero, 1)
            link(nc.vector.memset(ew_f[:, COLS:], 0.0))
            dve.wait_ge(s_edges, 64)
            dve.wait_ge(s_const, 8)
            for d in range(2):
                key = (dst_i, src_i)[d]
                other = (src_i, dst_i)[d]
                link(nc.vector.tensor_scalar(tmp_i[:, 0, :], key, P - 1, None, ALU.bitwise_and))
                link(nc.vector.tensor_copy(rec[d][:, :, 0], tmp_i[:, 0, :]))
                link(nc.vector.tensor_scalar(rec[d][:, :, 1], rel_i, float(NP), float(d * R * NP), ALU.mult, ALU.add))
                link(nc.vector.tensor_tensor(rec[d][:, :, 1], rec[d][:, :, 1], other, ALU.add))
                if d == 0:
                    link(nc.vector.tensor_copy(rec[0][:, :, 2], ew_f[:, 0:COLS]))
                link(nc.vector.tensor_scalar(tmp_i[:, 1, :], key, 7, None, ALU.logical_shift_right))
                link(nc.vector.tensor_tensor(onehotT, tile_no[:, :].unsqueeze(2).to_broadcast([P, TILES, COLS]),
                                             tmp_i[:, 1:2, :].to_broadcast([P, TILES, COLS]), ALU.is_equal))
                flat = onehotT.rearrange("p t j -> p (t j)")
                link(nc.vector.tensor_tensor_scan(runcount.rearrange("p t j -> p (t j)"), flat, flat, 0.0,
                                                  ALU.add, ALU.max))
                start = cnt[:, 1, :]
                link(nc.vector.memset(start, 0.0))
                link(nc.vector.tensor_copy(cnt[:, 1, 1:TILES], runcount[:, 0:TILES - 1, COLS - 1]))
                nc.vector.tensor_tensor(cnt[:, 0, :], runcount[:, :, COLS - 1], start, ALU.subtract).then_inc(s_cnt, 1)
                dve.wait_ge(s_cnt, d + 1)
                link(nc.vector.tensor_tensor(runcount, runcount, onehotT, ALU.mult))
                link(nc.vector.tensor_reduce(posf, runcount.rearrange("p t j -> p j t"), AX.X, ALU.add))
                dve.wait_ge(s_tot, d + 1)
                link(nc.vector.tensor_scalar(cnt_i[:, :], ps_cnt[:, 32:32 + TILES], float(PAIR - 1), None, ALU.add))
                link(nc.vector.tensor_scalar(cnt_i[:, :], cnt_i[:, :], 8, None, ALU.logical_shift_right))
                link(nc.vector.tensor_copy(cnt[:, 2, :], cnt_i[:, :]))
                link(nc.vector.tensor_tensor_scan(cnt[:, 3, :], cnt[:, 2, :], cnt[:, 2, :], 0.0, ALU.add, ALU.max))
                link(nc.vector.tensor_tensor(cnt[:, 4, :], cnt[:, 3, :], cnt[:, 2, :], ALU.subtract))
                link(nc.vector.scalar_tensor_tensor(out=cnt[:, 5, :], in0=cnt[:, 4, :], scalar=float(PAIR),
                                                    in1=ps_cnt[:, 0:TILES], op0=ALU.mult, op1=ALU.add))
                link(nc.vector.scalar_tensor_tensor(out=cnt[:, 6, :], in0=cnt[:, 5, :], scalar=-1.0,
                                                    in1=start, op0=ALU.add, op1=ALU.subtract))
                for t in range(TILES):
                    link(nc.vector.scalar_tensor_tensor(out=posf, in0=onehotT[:, t, :], scalar=cnt[:, 6, t:t + 1],
                                                        in1=posf, op0=ALU.mult, op1=ALU.add))
                link(nc.vector.tensor_copy(place[d], posf))
                link(nc.vector.tensor_scalar(tmp_i[:, 0, :], place[d], P - 1, None, ALU.bitwise_and))
                link(nc.vector.tensor_scalar(tmp_i[:, 1, :], place[d], 7, None, ALU.logical_shift_right))
                nc.vector.scalar_tensor_tensor(out=place[d], in0=tmp_i[:, 0, :], scalar=float(CH),
                                               in1=tmp_i[:, 1, :], op0=ALU.mult, op1=ALU.add).then_inc(s_place, 1)
                dve.wait_ge(s_place, d + 1)
                link(nc.vector.tensor_scalar(pair_tile[d], pair_no[:, :], cnt[:, 3, 0:1], None, ALU.is_ge))
                for t in range(1, TILES - 1):
                    link(nc.vector.scalar_tensor_tensor(out=pair_tile[d], in0=pair_no[:, :],
                                                        scalar=cnt[:, 3, t:t + 1], in1=pair_tile[d],
                                                        op0=ALU.is_ge, op1=ALU.add))
                row = 32 * d
                link(nc.vector.tensor_scalar(off512[d], pair_tile[d][row:row + 1, :], float(D), None, ALU.mult))

            mine = cell[:, 0:COLS]
            link(nc.vector.tensor_copy(cell[:, COLS:], nowhere[:, :].to_broadcast([P, ACOLS - COLS])))
            link(nc.vector.tensor_scalar(tmp_i[:, 0, :], dst_i, 7, None, ALU.logical_shift_right))
            link(nc.vector.tensor_scalar(tmp_i[:, 1, :], src_i, P - 1, None, ALU.bitwise_and))
            link(nc.vector.scalar_tensor_tensor(out=mine, in0=tmp_i[:, 0, :], scalar=float(P), in1=tmp_i[:, 1, :],
                                                op0=ALU.mult, op1=ALU.add))
            link(nc.vector.tensor_scalar(tmp_i[:, 0, :], src_i, 7, None, ALU.logical_shift_right))
            link(nc.vector.tensor_scalar(tmp_i[:, 1, :], dst_i, P - 1, None, ALU.bitwise_and))
            link(nc.vector.scalar_tensor_tensor(out=mine, in0=mine, scalar=float(TILES), in1=tmp_i[:, 0, :],
                                                op0=ALU.mult, op1=ALU.add))
            nc.vector.scalar_tensor_tensor(out=mine, in0=mine, scalar=float(P), in1=tmp_i[:, 1, :],
                                           op0=ALU.mult, op1=ALU.add).then_inc(s_cell, 1)

            dve.wait_ge(s_w[0], 32)
            for t in range(TILES):
                dve.wait_ge(s_hmm, t + 1)
                nc.vector.tensor_tensor(acc[:, t * D:(t + 1) * D], psum[t % BANKS][:, :], bias[:, 0], ALU.add).then_inc(s_hev, 1)

            def body(i):
                for h in range(2):
                    dve.wait_ge(s_w[1 - h], 32 * (i + 1 + h))
                    for t in range(TILES):
                        m = TILES + (i * 2 + h) * TILES + t
                        bank = (h * TILES + t) % BANKS
                        b = (h * BATCHES + t // BATCH)
                        dve.wait_ge(s_hmm, m + 1)
                        if t % BATCH == 0 and (later(i) or b >= 2):
                            dve.wait_ge(s_hst[b % 2], 16 * (i * BATCHES + b // 2))
                        nc.vector.tensor_tensor(stage[:, b % 2, t % BATCH, :], psum[bank][:, :], bias[:, 1 - h],
                                                ALU.add).then_inc(s_hev, 1)
            dve.wait_ge(s_padded, 32)
            loop(dve, R, body)

            dve.wait_ge(s_list[0], 16)
            nc.vector.tensor_copy(row_h[0], list0[:, :, 1]).then_inc(passes[0].ready, 1)
            dve.wait_ge(s_list[1], 16)
            nc.vector.tensor_copy(row_h[1], list1[:, :, 1]).then_inc(passes[1].ready, 1)

            def run_pass(ps):
                first = ps.n * HALVES

                def hots(i, h):
                    which = (ps.lst[:, bass.ds(i * SLOTS + h * HALF, HALF), 0:1]).to_broadcast([P, HALF, P])
                    lanes = lane[:, :].unsqueeze(1).to_broadcast([P, HALF, P])
                    if later(i):
                        dve.wait_ge(ps.prod, (i * 2 + h - 1) * HPAIRS)
                    nc.vector.tensor_tensor(onehot[:, h], lanes, which, ALU.is_equal).then_inc(ps.hot, 1)

                def compare(i, h):
                    g = first + i * 2 + h
                    dve.wait_ge(s_spread, g + 1)
                    if later(i) or ps.n:
                        dve.wait_ge(s_sum, g - 1)
                        dve.wait_ge(s_nw, g - 1)
                        dve.wait_ge(s_rank, AHALF * (g - 1))
                    for k in range(AHALF):
                        spread = ps_spread[h][:, k * P:(k + 1) * P]
                        own = cell[:, bass.ds(g * AHALF + k, 1)]
                        nc.vector.tensor_scalar(equal[:, h, k, :], spread, own, None, ALU.is_equal).then_inc(s_equal, 1)
                        nc.vector.scalar_tensor_tensor(out=earlier[:, h, k, :], in0=spread, scalar=own, in1=after[:, :],
                                                       op0=ALU.is_equal, op1=ALU.mult,
                                                       accum_out=rank[:, h, k:k + 1]).then_inc(s_rank, 1)

                def cells(i, h):
                    g = first + i * 2 + h
                    dve.wait_ge(s_rank, AHALF * (g + 1))
                    if later(i) or ps.n:
                        dve.wait_ge(s_acell, g - 1)
                    nc.vector.tensor_scalar(to_nowhere[:, h, :], rank[:, h, :], 0.0, nowhere[:, 0:1],
                                            ALU.is_gt, ALU.mult).then_inc(s_nw, 1)
                    dve.wait_ge(s_nw, g + 1)
                    if later(i) or ps.n:
                        dve.wait_ge(s_added, 16 * AHALF * (g - 1))
                    nc.vector.tensor_tensor(acell[:, h, :], to_nowhere[:, h, :], cell[:, bass.ds(g * AHALF, AHALF)],
                                            ALU.max).then_inc(s_acell, 1)

                def adds(i, h):
                    lo = (i * 2 + h) * HPAIRS
                    _, offs = nc.values_load_multi_w_load_instructions(
                        ps.off[:, bass.ds(lo, HPAIRS)], DVE_ONLY, min_val=0, max_val=(TILES - 1) * D,
                        skip_runtime_bounds_check_because="a pair's tile is a count of at most TILES - 1 comparisons")
                    for k in range(HPAIRS):
                        dest = acc[:, bass.ds(offs[k], D)]
                        dve.wait_ge(ps.prod, lo + k + 1)
                        if later(i) or h or k:
                            dve.wait_ge(ps.added, lo + k)
                        nc.vector.tensor_tensor(dest, psum[h * HPAIRS + k][:, :], dest, ALU.add).then_inc(ps.added, 1)

                def body(i):
                    if not later(i):
                        hots(0, 0)
                        compare(0, 0)
                        cells(0, 0)
                    for h in range(2):
                        if after_half(i, h):
                            hots(*after_half(i, h))
                            compare(*after_half(i, h))
                        adds(i, h)
                        if after_half(i, h):
                            cells(*after_half(i, h))
                loop(dve, LOOPS, body)
                dve.wait_ge(ps.added, PAIRS)

            run_pass(passes[0])
            run_pass(passes[1])

            dve.wait_ge(passes[0].dcol, HALVES)
            for t in range(TILES):
                link(nc.vector.scalar_tensor_tensor(out=degwork, in0=degmask[:, :], scalar=float(t),
                                                    in1=degpart, op0=ALU.is_equal, op1=ALU.mult))
                link(nc.vector.tensor_reduce(deg[:, 0, t:t + 1], degwork, AX.X, ALU.add))
            link(nc.vector.tensor_scalar(deg[:, 0, :], deg[:, 0, :], 1.0, None, ALU.add))
            nc.vector.tensor_scalar(deg[:, 1, :], deg[:, 0, :], TINY, None, ALU.max).then_inc(s_dv, 1)

            def norm(t0, ready):
                for t in range(TILES):
                    dve.wait_ge(s_res, t0 + t + 1)
                    nc.vector.bn_stats(stats[:, t, :], acc[:, t * D:(t + 1) * D]).then_inc(s_bn, 1)
                for t in range(TILES):
                    dve.wait_ge(s_bn, t0 + t + 1)
                    nc.vector.bn_aggr(mv[:, t, :], stats[:, t, :]).then_inc(s_mv, 1)
                dve.wait_ge(s_sd, ready)
                nc.vector.reciprocal(rstd[:, 1, :], rstd[:, 0, :]).then_inc(s_rs, 1)
                dve.wait_ge(s_rs, 1 if t0 == 0 else 2)
                for t in range(TILES):
                    nc.vector.tensor_scalar(acc[:, t * D:(t + 1) * D], acc[:, t * D:(t + 1) * D], mv[:, t, 0:1],
                                            rstd[:, 1, t:t + 1], ALU.subtract, ALU.mult).then_inc(s_x1, 1)

            for t in range(TILES):
                if t == TILES - 1:
                    dve.wait_ge(s_res, t - 3)
                    nc.vector.memset(xrow[64:P, t % 4], 0.0).then_inc(s_yv, 1)
                dve.wait_ge(s_x[t % 4], 16 * (t // 4 + 1))
                a = acc[:, t * D:(t + 1) * D]
                nc.vector.scalar_tensor_tensor(out=a, in0=a, scalar=0.0, in1=xrow[:, t % 4],
                                               op0=ALU.max, op1=ALU.add).then_inc(s_res, 1)
            norm(0, 2)
            link(nc.vector.reciprocal(deg[:, 1, :], deg[:, 2, :]))
            link(nc.vector.scalar_tensor_tensor(out=dinv, in0=deg[:, 0, :], scalar=0.0, in1=deg[:, 1, :],
                                                op0=ALU.is_gt, op1=ALU.mult))
            for t in range(TILES):
                dve.wait_ge(s_c1, t + 1)
                nc.vector.tensor_scalar(sent[:, t, :], psum[2 + t % 2][:, 0:DH], dinv[:, t:t + 1],
                                        None, ALU.mult).then_inc(s_hs, 1)
            for t in range(TILES):
                z = hidden[:, t, :]
                dve.wait_ge(s_conv, t + 1)
                dve.wait_ge(s_hs, t + 1)
                nc.vector.tensor_tensor(z, psum[4 + t % 2][:, 0:DH], sent[:, t, :], ALU.add).then_inc(s_z, 1)
                dve.wait_ge(s_z, 2 * t + 1)
                nc.vector.scalar_tensor_tensor(out=z, in0=z, scalar=dinv[:, t:t + 1], in1=b1s,
                                               op0=ALU.mult, op1=ALU.add).then_inc(s_z, 1)
                dve.wait_ge(s_z, 2 * t + 2)
                nc.vector.tensor_scalar(z, z, 0.0, dinv[:, t:t + 1], ALU.max, ALU.mult).then_inc(s_zz, 1)
            for t in range(TILES):
                dve.wait_ge(s_conv, TILES + t + 1)
                dve.wait_ge(s_zz, t + 1)
                nc.vector.tensor_tensor(sent[:, t, :], psum[4 + t % 2][:, 0:DH], hidden[:, t, :], ALU.add).then_inc(s_last, 1)
            dve.wait_ge(s_b12, 64)
            dve.wait_ge(s_last, TILES)
            for t in range(TILES):
                dve.wait_ge(s_c1, TILES + t + 1)
                nc.vector.scalar_tensor_tensor(out=y[:, t, :], in0=psum[2 + t % 2][:, :], scalar=dinv[:, t:t + 1],
                                               in1=b2s, op0=ALU.mult, op1=ALU.add).then_inc(s_yv, 1)
            dve.wait_ge(s_sq, TILES)
            nc.vector.tensor_scalar(cnt[:, 1, :], cnt[:, 0, :], TINY, None, ALU.max).then_inc(s_sq, 1)
            dve.wait_ge(s_sq, TILES + 2)
            link(nc.vector.tensor_scalar(cnt[:, 3, :], cnt[:, 2, :], EPS_NORM, None, ALU.max))
            link(nc.vector.reciprocal(cnt[:, 4, :], cnt[:, 3, :]))
            for t in range(TILES):
                a = acc[:, t * D:(t + 1) * D]
                nc.vector.scalar_tensor_tensor(out=a, in0=y[:, t, :], scalar=cnt[:, 4, t:t + 1], in1=a,
                                               op0=ALU.mult, op1=ALU.add).then_inc(s_res, 1)
            norm(TILES, 3)

        @block.tensor
        def _(pe):
            for d in range(2):
                pe.wait_ge(s_cnt, d + 1)
                nc.tensor.matmul(ps_cnt[:, 0:TILES], before[:, :], cnt[:, 0, :], start=True, stop=True)
                nc.tensor.matmul(ps_cnt[:, 32:32 + TILES], ones[:, :], cnt[:, 0, :], start=True, stop=True).then_inc(s_tot, 1)

            pe.wait_ge(s_xT, 16)
            pe.wait_ge(s_dx, 1)
            pe.wait_ge(s_w[0], 32)
            for t in range(TILES):
                if t >= BANKS:
                    pe.wait_ge(s_hev, t - BANKS + 1)
                for k in range(KD):
                    mm = nc.tensor.matmul(psum[t % BANKS][:, :], xTs[:, k, t * P:(t + 1) * P], wbuf[:, 0, k, :],
                                          start=(k == 0), stop=(k == KD - 1))
                mm.then_inc(s_hmm, 1)

            def body(i):
                for h in range(2):
                    pe.wait_ge(s_w[1 - h], 32 * (i + 1 + h))
                    for t in range(TILES):
                        m = TILES + (i * 2 + h) * TILES + t
                        bank = (h * TILES + t) % BANKS
                        pe.wait_ge(s_hev, m - BANKS + 1)
                        for k in range(KD):
                            mm = nc.tensor.matmul(psum[bank][:, :], xTs[:, k, t * P:(t + 1) * P],
                                                  wbuf[:, 1 - h, k, :], start=(k == 0), stop=(k == KD - 1))
                        mm.then_inc(s_hmm, 1)
            loop(pe, R, body)
            pe.wait_ge(s_hev, (2 * R + 1) * TILES)

            def run_pass(ps):
                first = ps.n * HALVES

                def spread(i, h):
                    g = first + i * 2 + h
                    pe.wait_ge(s_diag, AHALF * (g + 1))
                    if later(i) or ps.n:
                        pe.wait_ge(s_asum, g - 1)
                    nc.tensor.matmul(ps_spread[h][:, 0:AHALF * P], ones[:, :],
                                     diag[:, h].rearrange("p k e -> p (k e)"), start=True, stop=True).then_inc(s_spread, 1)

                def sums(i, h):
                    g = first + i * 2 + h
                    pe.wait_ge(s_equal, AHALF * (g + 1))
                    pe.wait_ge(s_rank, AHALF * (g + 1))
                    for k in range(AHALF):
                        mm = nc.tensor.matmul(ps_spread[h][:, SUMS + k:SUMS + k + 1], equal[:, h, k, :],
                                              ew_f[:, bass.ds(g * AHALF + k, 1)], start=True, stop=True)
                    mm.then_inc(s_sum, 1)

                def body(i):
                    if not later(i):
                        spread(0, 0)
                    for h in range(2):
                        if after_half(i, h):
                            spread(*after_half(i, h))
                        sums(i, h)
                        pe.wait_ge(ps.hot, i * 2 + h + 1)
                        if ps.degree and later(i):
                            pe.wait_ge(ps.dcol, i * 2 + h - 1)
                        for k in range(HPAIRS):
                            bank = h * HPAIRS + k
                            if later(i):
                                pe.wait_ge(ps.added, i * 2 * HPAIRS - 2 * HPAIRS + bank + 1)
                            for half_pair in range(2):
                                slot = 2 * bank + half_pair
                                hot = onehot[:, h, 2 * k + half_pair, :]
                                pe.wait_ge(ps.got[slot], 16 * (i + 1))
                                if ps.degree:
                                    nc.tensor.matmul(ps_deg[h][:, k:k + 1], hot,
                                                     list0[:, bass.ds(i * SLOTS + slot, 1), 2:3].rearrange("p a b -> p (a b)"),
                                                     start=(half_pair == 0), stop=(half_pair == 1))
                                mm = nc.tensor.matmul(psum[bank][:, :], hot, gathered[:, slot, :],
                                                      start=(half_pair == 0), stop=(half_pair == 1))
                            mm.then_inc(ps.prod, 1)
                loop(pe, LOOPS, body)

            pe.wait_ge(s_cell, 1)
            run_pass(passes[0])
            run_pass(passes[1])

            def convolve(source, n):
                for t in range(TILES):
                    m = n * TILES + t
                    if m >= 2:
                        pe.wait_ge(*((s_z, 2 * m - 3) if m - 2 < TILES else (s_last, m - 1 - TILES)))
                    pe.wait_ge(s_m[m % 3], 16 * (m // 3 + 1))
                    for k in range(TILES):
                        mm = nc.tensor.matmul(psum[4 + t % 2][:, 0:DH], mbuf[m % 3][:, k * P:(k + 1) * P],
                                              source[:, k, :], start=(k == 0), stop=(k == TILES - 1))
                    mm.then_inc(s_conv, 1)

            def transpose_and_multiply(source, blocks, weight, width, ready, base, column):
                def multiply(t):
                    pe.wait_ge(s_tpc, base + t + 1)
                    if t >= 2:
                        pe.wait_ge(*column(t - 2))
                    for k in range(blocks):
                        mm = nc.tensor.matmul(psum[2 + t % 2][:, 0:width], xt1[:, t % 2, k * P:(k + 1) * P],
                                              weight[:, k, :], start=(k == 0), stop=(k == blocks - 1))
                    mm.then_inc(s_c1, 1)
                for t in range(TILES):
                    if ready is not None:
                        pe.wait_ge(ready, t + 1)
                    if t >= 2:
                        pe.wait_ge(s_tpc, base + t - 1)
                    for k in range(blocks):
                        lo = (t * blocks + k) * P
                        mm = nc.tensor.transpose(psum[t % 2][:, k * P:(k + 1) * P], source[:, lo:lo + P], ident[:, :])
                    mm.then_inc(s_tp, 1)
                    if t:
                        multiply(t - 1)
                multiply(TILES - 1)

            pe.wait_ge(s_b12, 64)
            pe.wait_ge(passes[1].added, PAIRS)
            transpose_and_multiply(acc, KD, w1s, DH, s_x1, 0, lambda t: (s_hs, t + 1))
            pe.wait_ge(s_hs, TILES)
            convolve(sent, 0)
            pe.wait_ge(s_zz, TILES)
            convolve(hidden, 1)
            transpose_and_multiply(region_r, KH, w2s, D, s_last, TILES, lambda t: (s_yv, t + 2))


def kernel(**inputs):
    import numpy as _np
    import concourse.bacc as _bacc
    from concourse import mybir as _mybir
    from concourse.bass_utils import run_bass_kernel_spmd as _run

    given = {k: _np.asarray(v) for k, v in inputs.items()}
    laid = [
        ("x", given["x"]), ("xT", given["x"].T),
        ("src", given["src"]), ("dst", given["dst"]), ("rel", given["edge_type_8"]), ("ew", given["edge_weight"]),
        ("wselfT", given["L0_gnn_W_self"].T), ("bself", given["L0_gnn_b_self"]),
        ("wrelT", _np.roll(given["L0_gnn_W_rel"], R, axis=0).transpose(0, 2, 1)),
        ("brel", _np.roll(given["L0_gnn_b_rel"], R, axis=0)),
        ("w1", given["L1_gnn_W1"]), ("b1", given["L1_gnn_b1"]),
        ("w2", given["L1_gnn_W2"]), ("b2", given["L1_gnn_b2"]),
    ]
    nc = _bacc.Bacc("TRN2", target_bir_lowering=False, num_devices=1)
    arrays, args = {}, []
    for name, a in laid:
        a = _np.ascontiguousarray(a)
        arrays[f"in_{name}_dram"] = a
        args.append(nc.dram_tensor(f"in_{name}_dram", a.shape, _mybir.dt.from_np(a.dtype), kind="ExternalInput").ap())
    args.append(nc.dram_tensor("out_0_dram", (N, D), _mybir.dt.float32, kind="ExternalOutput").ap())
    build(nc, *args)
    r = _run(nc, [arrays], core_ids=[0])
    return r.results[0]["out_0_dram"]
```

```python
import concourse.bass as bass
from concourse import mybir
from contextlib import ExitStack

F32 = mybir.dt.float32
F32R = mybir.dt.float32r
F16 = mybir.dt.float16
I32 = mybir.dt.int32
ALU = mybir.AluOpType
ACT = mybir.ActivationFunctionType
DVE_ONLY = [mybir.EngineType.DVE]

P = 128
N = 2500
E = 80000
D = 512
KD = D // P
DH = 256
KH = DH // P
R = 8
TILES = -(-N // P)
NP = TILES * P
LAST = N - (TILES - 1) * P
COLS = E // P

GROUP = 5
GROUPS = 5
SCATTER_LOOPS = COLS // (GROUP * GROUPS)

SLOTS = 8
HALF = SLOTS // 2
MOST = (E + TILES * (P - 1)) // P
LOOPS = -(-MOST // SLOTS)
HALVES = 2 * LOOPS
CH = LOOPS * SLOTS
AHALF = 2
ATURNS = -(-COLS // (2 * AHALF))
DEGREE_TURNS = [0, ATURNS - LOOPS - 1]
ACOLS = 2 * AHALF * ATURNS
CELLS = NP * NP

BANKS = 4
BATCH = 4
BATCHES = TILES // BATCH
EPS_LN = 1e-5
EPS_NORM = 1e-12
GROUP1 = 2
LEAD = 3 * GROUP1
GROUP2 = 2
YRING = 2 * GROUP2
PIECES = 2
PBLOCKS = TILES // PIECES
PIECE = PBLOCKS * P
NPIECES = 2 * TILES * PIECES
RAWS = 5
HIGHS = 3
AHEAD = 3
TINY = 2.0 ** -116



class Pass:

    def __init__(self, n, lst, row, off, degree, ready, idx, got, hot, prod, added, dcol):
        self.n, self.lst, self.row, self.off, self.degree = n, lst, row, off, degree
        self.ready, self.idx, self.got, self.hot = ready, idx, got, hot
        self.prod, self.added, self.dcol = prod, added, dcol


def build(nc, x, xT, src, dst, rel, ew, wselfT, bself, wrelT, brel, w1, b1, w2, b2, out):
    ctx = ExitStack()
    with ctx:
        def sb(name, shape, dt=F32):
            return ctx.enter_context(nc.sbuf_tensor(name, shape, dt))

        def sem(name):
            return ctx.enter_context(nc.semaphore(name))

        tableH = nc.dram_tensor("tableH", [2 * R * NP, D], F32)
        matrix = nc.dram_tensor("matrix", [CELLS + P, 1], F32)
        WORDS = (3, 2)
        sorted_dram = [nc.dram_tensor(f"sorted{d}", [P * CH, WORDS[d]], F32) for d in range(2)]

        with ExitStack() as over:
            def view(name, columns, dt=F32R):
                return over.enter_context(nc.sbuf_tensor(name, [P, columns], dt))
            high = view("high", TILES * DH)[:, :].rearrange("p (t f) -> p t f", t=TILES)
            low_first = view("low_first", SLOTS * D)[:, :].rearrange("p (t f) -> p t f", f=DH)
            low_last = view("low_last", 4 * DH)[:, :].rearrange("p (t f) -> p t f", f=DH)
            view("rest_of_region_s", 2 * BATCH * D - 4 * DH, F32)
            piece_lo = view("piece_lo", RAWS * PIECE)[:, :].rearrange("p (b c) -> p b c", b=RAWS)
            piece_hi = view("piece_hi", HIGHS * PIECE)[:, :].rearrange("p (b c) -> p b c", b=HIGHS)
        region_r = sb("region_r", [P, TILES * DH])
        gathered = sb("gathered", [P, SLOTS, D])
        region_s = sb("region_s", [P, 2 * BATCH * D])
        region_x = sb("region_x", [P, KD * NP])
        region_acc = sb("region_acc", [P, 12500])
        onehotT = region_acc[:, 0:6250].bitcast(F16).rearrange("p (t j) -> p t j", t=TILES)
        runcount = region_acc[:, 6250:12500].bitcast(F16).rearrange("p (t j) -> p t j", t=TILES)
        acc = region_acc[:, 0:TILES * D]
        xTs = region_x[:, :].rearrange("p (k n) -> p k n", k=KD)
        piece = region_x[:, 0:RAWS * PIECE].rearrange("p (b c) -> p b c", b=RAWS)
        region_w = sb("region_w", [P, 2 * KD * D])
        wbuf = region_w[:, :].rearrange("p (b k o) -> p b k o", b=2, k=KD)
        w1s = region_w[:, 0:KD * DH].rearrange("p (k o) -> p k o", k=KD)
        w2s = region_w[:, KD * DH:2 * KD * DH].rearrange("p (k o) -> p k o", k=KH)
        xt1 = region_w[:, 2 * KD * DH:2 * KD * DH + 2 * D].rearrange("p (b f) -> p b f", b=2)
        b1s = region_w[:, 2 * KD * DH + 2 * D:2 * KD * DH + 2 * D + DH]
        b2s = region_w[:, 2 * KD * DH + 2 * D + DH:2 * KD * DH + 3 * D + DH]
        stage = region_s[:, :].rearrange("p (b t o) -> p b t o", b=2, t=BATCH)
        xrow = region_s[:, 0:4 * D].rearrange("p (b f) -> p b f", b=4)
        conv2 = region_s[:, 4 * DH:6 * DH].rearrange("p (b f) -> p b f", b=2)
        y = region_s[:, 4 * D:(4 + YRING) * D].rearrange("p (b f) -> p b f", b=YRING)
        edges = sb("edges", [P, 3 * CH + 8])
        src_i = edges[:, 0:COLS].bitcast(I32)
        dst_i = edges[:, COLS:2 * COLS].bitcast(I32)
        rel_i = edges[:, 2 * COLS:3 * COLS].bitcast(I32)
        list1 = edges[:, 0:2 * CH].rearrange("p (c w) -> p c w", w=2)
        ew_f = sb("ew_f", [P, ACOLS])
        cell = sb("cell", [P, ACOLS])
        scratch = sb("scratch", [P, 3, CH])
        tmp_i = scratch[:, 0:2, 0:COLS].bitcast(I32)
        posf = scratch[:, 2, 0:COLS]
        tile_h = posf.bitcast(F16)[:, 0:COLS]
        degwork = scratch[:, 0, 0:CH]
        degpart = scratch[:, 2, 0:CH]
        rec = [region_r[:, 0:3 * COLS].rearrange("p (j w) -> p j w", w=3),
               region_r[:, 3 * COLS:5 * COLS].rearrange("p (j w) -> p j w", w=2)]
        place = [region_r[:, (6 + d) * COLS:(7 + d) * COLS].bitcast(I32) for d in range(2)]
        place_st = sb("place_st", [P, GROUPS, GROUP], I32)
        rec_st = sb("rec_st", [P, GROUPS, GROUP, 3])
        list0 = sb("list0", [P, CH, 3])
        row_h = [scratch[:, 1, :].bitcast(I32), edges[:, 2 * CH:3 * CH].bitcast(I32)]
        idx_ring = sb("idx_ring", [P, 2, HALF], I32)
        zeros = gathered[:, :, :].rearrange("p s f -> p (s f)")[:, 0:NP]
        chunk_no = gathered[:, :, :].rearrange("p s f -> p (s f)")[:, NP:NP + CH]
        onehot = sb("onehot", [P, 2, HALF, P])

        def rows(t):
            place_of = [list0[:, :, :].rearrange("p c w -> p (c w)"), edges[:, :],
                        scratch[:, :, :].rearrange("p a c -> p (a c)")][t // 7]
            return place_of[:, (t % 7) * DH:(t % 7 + 1) * DH]

        def low(t):
            return low_first[:, t, :] if t < TILES - 4 else low_last[:, t - (TILES - 4), :]
        squares = onehot[:, :, :, :].rearrange("p h k f -> p h (k f)")
        bias = sb("bias", [P, 2, D])
        diag = sb("diag", [P, 2, AHALF, P])
        equal = sb("equal", [P, 2, AHALF, P])
        earlier = sb("earlier", [P, 2, AHALF, P], F16)
        rank = sb("rank", [P, 2, AHALF])
        nowhere = sb("nowhere", [P, 1])
        to_nowhere = sb("to_nowhere", [P, 2, AHALF])
        acell = sb("acell", [P, 2, AHALF], I32)
        asum = sb("asum", [P, 2, AHALF])
        ident = sb("ident", [P, P])
        before = sb("before", [P, P])
        after = sb("after", [P, P])
        ones = sb("ones", [P, P])
        lane = sb("lane", [P, P])
        tile_no = sb("tile_no", [P, TILES], F16)
        degmask = sb("degmask", [P, CH])
        chunk_tile = [degmask[:, :], scratch[:, 0, 0:CH]]
        offsets = sb("offsets", [P, CH], I32)
        off512 = [offsets[0:1, :], offsets[32:33, :]]
        cnt = sb("cnt", [P, 8, TILES])
        cnt_i = sb("cnt_i", [P, TILES], I32)
        deg = sb("deg", [P, 4, TILES])
        dinv = deg[:, 3, :]
        stats = sb("stats", [P, TILES, 6])
        mv = sb("mv", [P, TILES, 2])
        rstd = sb("rstd", [P, 3, TILES])
        epsc = sb("epsc", [P, 1])

        psum = [ctx.enter_context(nc.psum_tensor(f"ps{i}", [P, 512], F32)) for i in range(8)]
        ps_spread, ps_deg, ps_cnt = (psum[4], psum[7]), (psum[5], psum[6]), psum[7]
        SUMS = AHALF * P

        s_edges = sem("s_edges")
        s_xT = sem("s_xT")
        s_w = [sem(f"s_w{b}") for b in range(2)]
        s_const = sem("s_const")
        s_const2 = sem("s_const2")
        s_pad = sem("s_pad")
        s_padded = sem("s_padded")
        s_d = sem("s_d")
        s_cnt = sem("s_cnt")
        s_tot = sem("s_tot")
        s_place = sem("s_place")
        s_staged0 = sem("s_staged0")
        s_dx = sem("s_dx")
        s_staged = sem("s_staged")
        s_scat = [sem(f"s_scat{g}") for g in range(GROUPS)]
        s_list = [sem(f"s_list{d}") for d in range(2)]
        s_hmm = sem("s_hmm")
        s_hev = sem("s_hev")
        s_hst = [sem(f"s_hst{b}") for b in range(2)]
        s_zero = sem("s_zero")
        s_zeroed = sem("s_zeroed")
        s_cell = sem("s_cell")
        s_diag = sem("s_diag")
        s_spread = sem("s_spread")
        s_equal = sem("s_equal")
        s_rank = sem("s_rank")
        s_nw = sem("s_nw")
        s_acell = sem("s_acell")
        s_sum = sem("s_sum")
        s_asum = sem("s_asum")
        s_added = sem("s_added")
        s_m = [sem(f"s_m{b}") for b in range(RAWS)]
        s_mh = sem("s_mh")
        s_ml = sem("s_ml")
        s_hi = sem("s_hi")
        s_lo = sem("s_lo")
        s_piece = sem("s_piece")
        s_last = sem("s_last")
        s_b12 = sem("s_b12")
        s_x = [sem(f"s_xrow{b}") for b in range(4)]
        s_res = sem("s_res")
        s_bn = sem("s_bn")
        s_mv = sem("s_mv")
        s_sd = sem("s_sd")
        s_rs = sem("s_rs")
        s_x1 = sem("s_x1")
        s_dsq = sem("s_dsq")
        s_xz = sem("s_xz")
        s_n1 = sem("s_n1")
        s_n2 = sem("s_n2")
        s_tp = sem("s_tp")
        s_tpc = sem("s_tpc")
        s_c1 = sem("s_c1")
        s_hs = sem("s_hs")
        s_z = sem("s_z")
        s_zz = sem("s_zz")
        s_dv = sem("s_dv")
        s_sq = sem("s_sq")
        s_out = sem("s_out")
        s_yv = sem("s_yv")

        s_ready = [sem(f"s_ready{d}") for d in range(2)]
        passes = []
        for n, (lst, row, off, degree) in enumerate([(list0, row_h[0], off512[0], True),
                                                     (list1, row_h[1], off512[1], False)]):
            passes.append(Pass(
                n=n, lst=lst, row=row, off=off, degree=degree,
                ready=s_ready[n],
                idx=sem(f"p{n}_idx"),
                got=[sem(f"p{n}_got{k}") for k in range(SLOTS)],
                hot=sem(f"p{n}_hot"),
                prod=sem(f"p{n}_prod"),
                added=sem(f"p{n}_added"),
                dcol=sem(f"p{n}_dcol")))

        block = ctx.enter_context(nc.Block())

        def loop(eng, count, body):
            body(0)
            with eng.Fori(1, count - 1) as i:
                body(i)
            body(count - 1)

        def loop_pass(eng, n, body):
            last = LOOPS if n == 0 else ATURNS - LOOPS
            body(0, True)
            with eng.Fori(1, last - 1) as i:
                body(i, True)
            body(last - 1, True)
            if last < LOOPS:
                with eng.Fori(last, LOOPS - 1) as i:
                    body(i, False)
                body(LOOPS - 1, False)

        def columns_at(n, half, columns):
            if half is None:
                return False
            return n * LOOPS + half[0] < ATURNS if isinstance(half[0], int) else columns

        def in_register(eng, value):
            return value if isinstance(value, int) else eng.to_reg(value)

        def later(i):
            return not (isinstance(i, int) and i == 0)

        def two_after(i, h):
            return None if isinstance(i, int) and i == LOOPS - 1 else (i + 1, h)

        def after_half(i, h):
            if h == 0:
                return i, 1
            return None if isinstance(i, int) and i == LOOPS - 1 else (i + 1, 0)

        @block.sync
        def _(sp):
            for a, v in ((src_i, src), (dst_i, dst), (rel_i, rel), (ew_f[:, 0:COLS], ew)):
                sp.dma_start(a, v.rearrange("(p j) -> p j", p=P)).then_inc(s_edges, 16)
            sp.wait_ge(s_pad, 2)
            sp.dma_start(sorted_dram[0].rearrange("(p c) w -> p (c w)", p=P),
                         list0[:, :, :].rearrange("p c w -> p (c w)")).then_inc(s_padded, 16)
            sp.dma_start(sorted_dram[1].rearrange("(p c) w -> p (c w)", p=P),
                         region_s[:, 0:2 * CH]).then_inc(s_padded, 16)
            sp.dma_start(xTs[:, :, 0:N], xT.rearrange("(k p) n -> p k n", p=P)).then_inc(s_xT, 16)
            sp.dma_start(wbuf[:, 0], wselfT.rearrange("(k p) o -> p k o", p=P)).then_inc(s_w[0], 16)
            sp.dma_start(bias[:, 0], bself[None, :].partition_broadcast(P)).then_inc(s_w[0], 16)
            wrel_v = wrelT.rearrange("r (k p) o -> r p k o", p=P)

            def load_w(slot, buf):
                sp.dma_start(wbuf[:, buf], wrel_v[bass.ds(slot, 1)].rearrange("a p k o -> p (a k) o")).then_inc(s_w[buf], 16)
                sp.dma_start(bias[:, buf], brel[bass.ds(slot, 1), :].partition_broadcast(P)).then_inc(s_w[buf], 16)

            load_w(0, 1)
            sp.wait_ge(s_zero, 1)
            for t in range(TILES):
                sp.wait_ge(s_hev, t + 1)
                sp.dma_start(matrix[t * P * NP:(t + 1) * P * NP, :].rearrange("(p c) w -> p (c w)", p=P),
                             zeros).then_inc(s_zeroed, 16)
            sp.dma_start(matrix[CELLS:CELLS + P, :], gathered[:, 0, 0:1]).then_inc(s_zeroed, 16)
            sp.wait_ge(s_hev, TILES)
            load_w(1, 0)
            table_v = tableH.rearrange("(s b t p) o -> s b p t o", s=2 * R, b=BATCHES, t=BATCH)

            def body(i):
                for h in range(2):
                    for b in range(BATCHES):
                        m = TILES + (i * 2 + h) * TILES + (b + 1) * BATCH
                        st = (h * BATCHES + b) % 2
                        sp.wait_ge(s_hev, m)
                        sp.dma_start(table_v[bass.ds(i * 2 + h, 1), b].rearrange("a p t o -> p (a t) o"),
                                     stage[:, st]).then_inc(s_hst[st], 16)
                    if isinstance(i, int) and i == R - 1:
                        continue
                    load_w(i * 2 + h + 2, 1 - h)

            loop(sp, R, body)
            sp.wait_ge(s_hmm, (2 * R + 1) * TILES)
            for b in range(2):
                sp.wait_ge(s_hst[b], 16 * R * BATCHES)
            sp.dma_start(w1s, w1.rearrange("(k p) o -> p k o", p=P)).then_inc(s_b12, 16)
            sp.dma_start(w2s, w2.rearrange("(k p) o -> p k o", p=P)).then_inc(s_b12, 16)
            sp.dma_start(b1s, b1[None, :].partition_broadcast(P)).then_inc(s_b12, 16)
            sp.dma_start(b2s, b2[None, :].partition_broadcast(P)).then_inc(s_b12, 16)
            def load_piece(j):
                t, part = (j // PIECES) % TILES, j % PIECES
                if j >= RAWS:
                    sp.wait_ge(s_piece, j - RAWS + 1)
                whole = matrix[t * P * NP:(t + 1) * P * NP, :].rearrange("(p c) w -> p (c w)", p=P)
                sp.dma_start(piece[:, j % RAWS, :], whole[:, part * PIECE:(part + 1) * PIECE]).then_inc(s_m[j % RAWS], 16)

            for t in range(TILES):
                m = P if t < TILES - 1 else LAST
                if t == 4:
                    sp.wait_ge(s_added, 16 * ACOLS)
                    for j in range(RAWS):
                        sp.wait_ge(passes[1].prod, CH - SLOTS * max(AHEAD - j, 0))
                        load_piece(j)
                if t >= 4:
                    sp.wait_ge(s_res, t - 3)
                if t == TILES - 1:
                    sp.wait_ge(s_xz, 1)
                sp.dma_start(xrow[0:m, t % 4], x[t * P:t * P + m, :]).then_inc(s_x[t % 4], 16)
            def store(t):
                m = P if t < TILES - 1 else LAST
                sp.wait_ge(s_x1, TILES + t + 1)
                sp.dma_start(out[t * P:t * P + m, :], acc[0:m, t * D:(t + 1) * D]).then_inc(s_out, 16)

            early = (TILES + 7) * PIECES
            for j in range(RAWS, NPIECES):
                load_piece(j)
                if j >= early and j % PIECES == 0:
                    store((j - early) // PIECES)
            for t in range((NPIECES - early) // PIECES, TILES):
                store(t)
            sp.wait_ge(s_out, 16 * TILES)

        @block.gpsimd
        def _(pool):
            nc.gpsimd.memset(ident[:, :], 0.0).then_inc(s_const2, 1)
            nc.gpsimd.memset(before[:, :], 1.0).then_inc(s_const2, 1)
            pool.wait_ge(s_const2, 2)
            nc.gpsimd.affine_select(out=ident[:, :], in_=ident[:, :], compare_op=ALU.not_equal, fill=1.0,
                                    base=0, pattern=[[-1, P]], channel_multiplier=1).then_inc(s_const, 1)
            nc.gpsimd.memset(after[:, :], 1.0).then_inc(s_const2, 1)
            pool.wait_ge(s_const2, 3)
            nc.gpsimd.affine_select(out=after[:, :], in_=after[:, :], compare_op=ALU.is_gt, fill=0.0,
                                    base=0, pattern=[[-1, P]], channel_multiplier=1).then_inc(s_const, 1)
            nc.gpsimd.iota(nowhere[:, :], [[1, 1]], base=CELLS, channel_multiplier=1,
                           allow_small_or_imprecise_dtypes=True).then_inc(s_const, 1)
            nc.gpsimd.affine_select(out=before[:, :], in_=before[:, :], compare_op=ALU.is_gt, fill=0.0,
                                    base=0, pattern=[[1, P]], channel_multiplier=-1).then_inc(s_const, 1)
            nc.gpsimd.memset(ones[:, :], 1.0).then_inc(s_const, 1)
            nc.gpsimd.iota(lane[:, :], [[1, P]], base=0, channel_multiplier=0,
                           allow_small_or_imprecise_dtypes=True).then_inc(s_const, 1)
            nc.gpsimd.iota(tile_no[:, :], [[1, TILES]], base=0, channel_multiplier=0,
                           allow_small_or_imprecise_dtypes=True).then_inc(s_const, 1)
            nc.gpsimd.iota(chunk_no, [[1, CH]], base=0, channel_multiplier=0,
                           allow_small_or_imprecise_dtypes=True).then_inc(s_const, 1)
            pool.wait_ge(s_padded, 32)
            for d in range(2):
                def body(i):
                    for g in range(GROUPS):
                        staged = in_register(pool, (d * SCATTER_LOOPS + i) * GROUPS + g + 1)
                        pool.wait_ge(s_padded, 32)
                        pool.wait_ge(s_staged, staged)
                        for k in range(GROUP):
                            pool.indirect_dma_start(
                                sorted_dram[d][:, :],
                                bass.IndirectOffsetOnAxis(ap=place_st[:, g, k:k + 1], axis=0),
                                rec_st[:, g, k, 0:WORDS[d]], None).then_inc(s_scat[g], 16)
                loop(pool, SCATTER_LOOPS, body)

            def add_column(turn, h, k):
                number = (turn * 2 + h) * AHALF + k
                cells = in_register(pool, turn * 2 + h + 1)
                before_it = in_register(pool, number * 16)
                pool.wait_ge(s_zeroed, 16 * (TILES + 1))
                pool.wait_ge(s_acell, cells)
                pool.wait_ge(s_asum, cells)
                if not (isinstance(number, int) and number == 0):
                    pool.wait_ge(s_added, before_it)
                pool.indirect_dma_start(
                    matrix[:, :], bass.IndirectOffsetOnAxis(ap=acell[:, h, k:k + 1], axis=0),
                    asum[:, h, k:k + 1], None, compute_op=ALU.add).then_inc(s_added, 16)

            for ps in passes:
                if ps.n == 0:
                    for b in range(2):
                        pool.wait_ge(s_hst[b], 16 * R * BATCHES)

                def body(i, columns, ps=ps):
                    for h in range(2):
                        half = in_register(pool, i * 2 + h + 1)
                        pool.wait_ge(ps.ready, 1)
                        pool.wait_ge(ps.idx, half)
                        for k in range(HALF):
                            slot = h * HALF + k
                            if ps.n and not later(i) and k % 2 == 0:
                                pool.wait_ge(passes[ps.n - 1].prod, CH - SLOTS + slot + 2)
                            if later(i) and k % 2 == 0:
                                done = in_register(pool, i * SLOTS - SLOTS + slot + 2)
                                pool.wait_ge(ps.ready, 1)
                                pool.wait_ge(ps.prod, done)
                            pool.indirect_dma_start(
                                gathered[:, slot, :], None, tableH[:, :],
                                bass.IndirectOffsetOnAxis(ap=idx_ring[:, h, k:k + 1], axis=0)).then_inc(ps.got[slot], 16)
                            if k % 2 and columns and (ps.n or later(i) or h):
                                turn = ps.n * LOOPS + i
                                add_column(turn if h else turn - 1, 1 - h, k // 2)
                    if isinstance(i, int) and ps.n * LOOPS + i == ATURNS - 1:
                        for k in range(AHALF):
                            add_column(ATURNS - 1, 1, k)
                loop_pass(pool, ps.n, body)

        @block.scalar
        def _(act):
            for d in range(2):
                act.wait_ge(s_place, d + 1)

                def body(i):
                    for g in range(GROUPS):
                        if later(i) or d:
                            act.wait_ge(s_scat[g], 16 * GROUP * (d * SCATTER_LOOPS + i))
                        col = (i * GROUPS + g) * GROUP
                        nc.scalar.copy(place_st[:, g, :], place[d][:, bass.ds(col, GROUP)]).then_inc(s_staged0, 1)
                        nc.scalar.copy(rec_st[:, g, :, 0:WORDS[d]], rec[d][:, bass.ds(col, GROUP), :]).then_inc(s_staged0, 1)
                        act.wait_ge(s_staged0, 2 * ((d * SCATTER_LOOPS + i) * GROUPS + g + 1))
                        act.sem_inc(s_staged, 1)
                loop(act, SCATTER_LOOPS, body)
                for g in range(GROUPS):
                    act.wait_ge(s_scat[g], 16 * GROUP * SCATTER_LOOPS * (d + 1))
                act.wait_ge(s_cell, 1)
                lst = (list0[:, :, :], list1)[d]
                act.dma_start(lst.rearrange("p c w -> p (c w)"),
                              sorted_dram[d].rearrange("(p c) w -> p (c w)", p=P)).then_inc(s_list[d], 16)

            pieces = [0]

            def piece_highs(count):
                while pieces[0] < min(count, NPIECES):
                    j = pieces[0]
                    act.wait_ge(s_m[j % RAWS], 16 * (j // RAWS + 1))
                    if j >= HIGHS:
                        act.wait_ge(s_piece, j - HIGHS + 1)
                    nc.scalar.copy(piece_hi[:, j % HIGHS, :], piece[:, j % RAWS, :]).then_inc(s_mh, 1)
                    pieces[0] += 1

            def run_pass(ps):
                act.wait_ge(ps.ready, 1)
                first = ps.n * HALVES

                def diagonals(i, h):
                    if later(i) or ps.n:
                        act.wait_ge(s_spread, first + i * 2 + h - 1)
                    for k in range(AHALF):
                        col = (first + i * 2 + h) * AHALF + k
                        nc.scalar.activation(diag[:, h, k, :], ident[:, :], ACT.Copy,
                                             scale=cell[:, bass.ds(col, 1)]).then_inc(s_diag, 1)

                def rows(i, h):
                    if later(i):
                        for k in range(HALF):
                            act.wait_ge(ps.got[h * HALF + k], 16 * i)
                    elif ps.n:
                        for k in range(HALF):
                            act.wait_ge(passes[ps.n - 1].got[h * HALF + k], 16 * LOOPS)
                    nc.scalar.copy(idx_ring[:, h, :], ps.row[:, bass.ds(i * SLOTS + h * HALF, HALF)]).then_inc(ps.idx, 1)

                def sums(i, h):
                    act.wait_ge(s_sum, first + i * 2 + h + 1)
                    if later(i) or ps.n:
                        act.wait_ge(s_added, 16 * AHALF * (first + i * 2 + h - 1))
                    nc.scalar.copy(asum[:, h, :], ps_spread[h][:, SUMS:SUMS + AHALF]).then_inc(s_asum, 1)

                def body(i, columns):
                    if not later(i):
                        rows(0, 0)
                        diagonals(0, 0)
                        diagonals(0, 1)
                    for h in range(2):
                        if columns_at(ps.n, two_after(i, h), columns):
                            diagonals(*two_after(i, h))
                        if after_half(i, h):
                            rows(*after_half(i, h))
                        if columns:
                            sums(i, h)
                        if ps.degree:
                            act.wait_ge(ps.prod, (i * 2 + h + 1) * HALF)
                            nc.scalar.copy(degpart[:, bass.ds((i * 2 + h) * HALF, HALF)],
                                           ps_deg[h][:, 0:HALF]).then_inc(ps.dcol, 1)
                        if ps.n and isinstance(i, int) and i == LOOPS - 1:
                            piece_highs(h + 1)
                loop_pass(act, ps.n, body)

            def transposes(t, blocks, base):
                act.wait_ge(s_tp, base + t + 1)
                if t >= 2 or base:
                    act.wait_ge(s_c1, base + t - 1)
                nc.scalar.copy(xt1[:, t % 2, 0:blocks * P], psum[t % 2][:, 0:blocks * P]).then_inc(s_tpc, 1)

            run_pass(passes[0])
            run_pass(passes[1])
            act.wait_ge(s_dv, 1)
            nc.scalar.activation(deg[:, 2, :], deg[:, 1, :], ACT.Sqrt).then_inc(s_dsq, 1)

            def deviations(g, size, base):
                lo, hi = g * size, (g + 1) * size
                act.wait_ge(s_mv, base + hi)
                nc.scalar.activation(rstd[:, 0, lo:hi], mv[:, lo:hi, 1], ACT.Sqrt,
                                     bias=epsc[:, 0:1]).then_inc(s_sd, 1)

            def normalise(t, group):
                act.wait_ge(s_rs, group + 1)
                a = acc[:, t * D:(t + 1) * D]
                nc.scalar.activation(a, a, ACT.Identity, scale=rstd[:, 1, t:t + 1],
                                     bias=rstd[:, 2, t:t + 1]).then_inc(s_x1, 1)

            def highs(t, ready, count):
                act.wait_ge(ready, count)
                nc.scalar.copy(high[:, t, :], rows(t)).then_inc(s_hi, 1)

            deviations(0, GROUP1, 0)
            for t in range(TILES):
                normalise(t, t // GROUP1)
                if t:
                    transposes(t - 1, KD, 0)
                if t % GROUP1 == 1 and t // GROUP1 + 1 < TILES // GROUP1:
                    deviations(t // GROUP1 + 1, GROUP1, 0)
                if t >= 3:
                    highs(t - 3, s_hs, t - 2)
                if t == TILES // 2:
                    piece_highs(AHEAD)
            transposes(TILES - 1, KD, 0)
            for t in range(TILES - 3, TILES):
                highs(t, s_hs, t + 1)
            for t in range(TILES):
                piece_highs(AHEAD + PIECES * (t + 1) - (t == TILES - 1))
            act.wait_ge(s_piece, TILES * PIECES)
            for t in range(TILES):
                highs(t, s_zz, t + 1)
                if t == TILES // 2:
                    piece_highs(AHEAD + PIECES * TILES)
            for step in range(TILES + 2):
                upto = AHEAD + PIECES * (TILES + step + 1)
                piece_highs(upto - 1)
                if 1 <= step < TILES:
                    transposes(step - 1, KH, TILES)
                piece_highs(upto)
                if step == TILES - 1:
                    transposes(step, KH, TILES)
                t = step - 2
                if t < 0:
                    continue
                act.wait_ge(s_yv, t + 1)
                nc.scalar.activation(squares[:, t % 2, :], y[:, t % YRING, :], ACT.Square,
                                     accum_out=cnt[:, 0, t:t + 1]).then_inc(s_sq, 1)
                if t % GROUP2 == GROUP2 - 1:
                    g = t // GROUP2
                    lo = g * GROUP2
                    piece_highs(upto + 1)
                    act.wait_ge(s_n1, g + 1)
                    nc.scalar.activation(cnt[:, 2, lo:t + 1], cnt[:, 1, lo:t + 1], ACT.Sqrt).then_inc(s_n2, 1)
                    deviations(g, GROUP2, TILES)
                    for tile in range(lo, t + 1):
                        normalise(tile, TILES // GROUP1 + g)

        @block.vector
        def _(dve):
            steps = [0]

            def link(ins):
                steps[0] += 1
                ins.then_inc(s_d, 1)
                dve.wait_ge(s_d, steps[0])

            link(nc.vector.memset(epsc[:, :], EPS_LN))
            link(nc.vector.memset(list0[:, :, :], 0.0))
            nc.vector.memset(list0[:, :, 0:1], -1.0).then_inc(s_pad, 1)
            link(nc.vector.memset(region_s[:, 0:2 * CH], 0.0))
            nc.vector.memset(region_s[:, 0:2 * CH].rearrange("p (c w) -> p c w", w=2)[:, :, 0:1], -1.0).then_inc(s_pad, 1)
            link(nc.vector.memset(ew_f[:, COLS:], 0.0))
            dve.wait_ge(s_edges, 64)
            dve.wait_ge(s_const, 8)
            for d in range(2):
                if d == 1:
                    nc.vector.memset(xTs[:, :, N:NP], 0.0).then_inc(s_dx, 1)
                    nc.vector.memset(zeros, 0.0).then_inc(s_zero, 1)
                key = (dst_i, src_i)[d]
                other = (src_i, dst_i)[d]
                link(nc.vector.tensor_scalar(tmp_i[:, 0, :], key, P - 1, None, ALU.bitwise_and))
                link(nc.vector.tensor_copy(rec[d][:, :, 0], tmp_i[:, 0, :]))
                link(nc.vector.tensor_scalar(rec[d][:, :, 1], rel_i, float(NP), float(d * R * NP), ALU.mult, ALU.add))
                link(nc.vector.tensor_tensor(rec[d][:, :, 1], rec[d][:, :, 1], other, ALU.add))
                if d == 0:
                    link(nc.vector.tensor_copy(rec[0][:, :, 2], ew_f[:, 0:COLS]))
                link(nc.vector.tensor_scalar(tmp_i[:, 1, :], key, 7, None, ALU.logical_shift_right))
                link(nc.vector.tensor_copy(tile_h, tmp_i[:, 1, :]))
                for t in range(TILES):
                    one = nc.vector.tensor_scalar(onehotT[:, t, :], tile_h, float(t), None, ALU.is_equal)
                link(one)
                flat = onehotT.rearrange("p t j -> p (t j)")
                link(nc.vector.tensor_tensor_scan(runcount.rearrange("p t j -> p (t j)"), flat, flat, 0.0,
                                                  ALU.add, ALU.max))
                start = cnt[:, 1, :]
                link(nc.vector.memset(start, 0.0))
                link(nc.vector.tensor_copy(cnt[:, 1, 1:TILES], runcount[:, 0:TILES - 1, COLS - 1]))
                nc.vector.tensor_tensor(cnt[:, 0, :], runcount[:, :, COLS - 1], start, ALU.subtract).then_inc(s_cnt, 1)
                dve.wait_ge(s_cnt, d + 1)
                link(nc.vector.tensor_tensor(runcount, runcount, onehotT, ALU.mult))
                left = TILES
                while left > 2:
                    half = left // 2
                    link(nc.vector.tensor_tensor(runcount[:, 0:half, :], runcount[:, 0:half, :],
                                                 runcount[:, left - half:left, :], ALU.add))
                    left -= half
                link(nc.vector.tensor_tensor(posf, runcount[:, 0, :], runcount[:, 1, :], ALU.add))
                dve.wait_ge(s_tot, d + 1)
                link(nc.vector.tensor_scalar(cnt_i[:, :], ps_cnt[:, 32:32 + TILES], float(P - 1), None, ALU.add))
                link(nc.vector.tensor_scalar(cnt_i[:, :], cnt_i[:, :], 7, None, ALU.logical_shift_right))
                link(nc.vector.tensor_copy(cnt[:, 2, :], cnt_i[:, :]))
                link(nc.vector.tensor_tensor_scan(cnt[:, 3, :], cnt[:, 2, :], cnt[:, 2, :], 0.0, ALU.add, ALU.max))
                link(nc.vector.tensor_tensor(cnt[:, 4, :], cnt[:, 3, :], cnt[:, 2, :], ALU.subtract))
                link(nc.vector.scalar_tensor_tensor(out=cnt[:, 5, :], in0=cnt[:, 4, :], scalar=float(P),
                                                    in1=ps_cnt[:, 0:TILES], op0=ALU.mult, op1=ALU.add))
                link(nc.vector.scalar_tensor_tensor(out=cnt[:, 6, :], in0=cnt[:, 5, :], scalar=-1.0,
                                                    in1=start, op0=ALU.add, op1=ALU.subtract))
                for t in range(TILES):
                    link(nc.vector.scalar_tensor_tensor(out=posf, in0=onehotT[:, t, :], scalar=cnt[:, 6, t:t + 1],
                                                        in1=posf, op0=ALU.mult, op1=ALU.add))
                link(nc.vector.tensor_copy(place[d], posf))
                link(nc.vector.tensor_scalar(tmp_i[:, 0, :], place[d], P - 1, None, ALU.bitwise_and))
                link(nc.vector.tensor_scalar(tmp_i[:, 1, :], place[d], 7, None, ALU.logical_shift_right))
                nc.vector.scalar_tensor_tensor(out=place[d], in0=tmp_i[:, 0, :], scalar=float(CH),
                                               in1=tmp_i[:, 1, :], op0=ALU.mult, op1=ALU.add).then_inc(s_place, 1)
                dve.wait_ge(s_place, d + 1)
                link(nc.vector.tensor_scalar(chunk_tile[d], chunk_no, cnt[:, 3, 0:1], None, ALU.is_ge))
                for t in range(1, TILES - 1):
                    link(nc.vector.scalar_tensor_tensor(out=chunk_tile[d], in0=chunk_no,
                                                        scalar=cnt[:, 3, t:t + 1], in1=chunk_tile[d],
                                                        op0=ALU.is_ge, op1=ALU.add))
                row = 32 * d
                link(nc.vector.tensor_scalar(off512[d], chunk_tile[d][row:row + 1, :], float(D), None, ALU.mult))

            mine = cell[:, 0:COLS]
            link(nc.vector.tensor_copy(cell[:, COLS:], nowhere[:, :].to_broadcast([P, ACOLS - COLS])))
            link(nc.vector.tensor_scalar(tmp_i[:, 0, :], dst_i, 7, None, ALU.logical_shift_right))
            link(nc.vector.tensor_scalar(tmp_i[:, 1, :], src_i, P - 1, None, ALU.bitwise_and))
            link(nc.vector.scalar_tensor_tensor(out=mine, in0=tmp_i[:, 0, :], scalar=float(P), in1=tmp_i[:, 1, :],
                                                op0=ALU.mult, op1=ALU.add))
            link(nc.vector.tensor_scalar(tmp_i[:, 0, :], src_i, 7, None, ALU.logical_shift_right))
            link(nc.vector.tensor_scalar(tmp_i[:, 1, :], dst_i, P - 1, None, ALU.bitwise_and))
            link(nc.vector.scalar_tensor_tensor(out=mine, in0=mine, scalar=float(TILES), in1=tmp_i[:, 0, :],
                                                op0=ALU.mult, op1=ALU.add))
            nc.vector.scalar_tensor_tensor(out=mine, in0=mine, scalar=float(P), in1=tmp_i[:, 1, :],
                                           op0=ALU.mult, op1=ALU.add).then_inc(s_cell, 1)

            dve.wait_ge(s_w[0], 32)
            for t in range(TILES):
                dve.wait_ge(s_hmm, t + 1)
                nc.vector.tensor_tensor(acc[:, t * D:(t + 1) * D], psum[t % BANKS][:, :], bias[:, 0], ALU.add).then_inc(s_hev, 1)

            def body(i):
                for h in range(2):
                    dve.wait_ge(s_w[1 - h], 32 * (i + 1 + h))
                    for t in range(TILES):
                        m = TILES + (i * 2 + h) * TILES + t
                        bank = (h * TILES + t) % BANKS
                        b = (h * BATCHES + t // BATCH)
                        dve.wait_ge(s_hmm, m + 1)
                        if t % BATCH == 0 and (later(i) or b >= 2):
                            dve.wait_ge(s_hst[b % 2], 16 * (i * BATCHES + b // 2))
                        nc.vector.tensor_tensor(stage[:, b % 2, t % BATCH, :], psum[bank][:, :], bias[:, 1 - h],
                                                ALU.add).then_inc(s_hev, 1)
            dve.wait_ge(s_padded, 32)
            loop(dve, R, body)

            dve.wait_ge(s_list[0], 16)
            nc.vector.tensor_copy(row_h[0], list0[:, :, 1]).then_inc(passes[0].ready, 1)
            dve.wait_ge(s_list[1], 16)
            nc.vector.tensor_copy(row_h[1], list1[:, :, 1]).then_inc(passes[1].ready, 1)

            pieces = [0]

            def piece_lows(count):
                while pieces[0] < min(count, NPIECES):
                    j = pieces[0]
                    dve.wait_ge(s_mh, j + 1)
                    nc.vector.tensor_tensor(piece_lo[:, j % RAWS, :], piece[:, j % RAWS, :],
                                            piece_hi[:, j % HIGHS, :].bitcast(F32), ALU.subtract).then_inc(s_ml, 1)
                    pieces[0] += 1

            def degrees(part, parts):
                if part == 0:
                    dve.wait_ge(passes[0].dcol, HALVES)
                for t in range(part * TILES // parts, (part + 1) * TILES // parts):
                    link(nc.vector.scalar_tensor_tensor(out=degwork, in0=degmask[:, :], scalar=float(t),
                                                        in1=degpart, op0=ALU.is_equal, op1=ALU.mult,
                                                        accum_out=deg[:, 0, t:t + 1]))
                if part == parts - 1:
                    link(nc.vector.tensor_scalar(deg[:, 0, :], deg[:, 0, :], 1.0, None, ALU.add))
                    nc.vector.tensor_scalar(deg[:, 1, :], deg[:, 0, :], TINY, None, ALU.max).then_inc(s_dv, 1)

            def run_pass(ps):
                first = ps.n * HALVES

                def hots(i, h):
                    which = (ps.lst[:, bass.ds(i * SLOTS + h * HALF, HALF), 0:1]).to_broadcast([P, HALF, P])
                    lanes = lane[:, :].unsqueeze(1).to_broadcast([P, HALF, P])
                    if later(i):
                        dve.wait_ge(ps.prod, (i * 2 + h - 1) * HALF)
                    nc.vector.tensor_tensor(onehot[:, h], lanes, which, ALU.is_equal).then_inc(ps.hot, 1)

                def compare(i, h):
                    g = first + i * 2 + h
                    dve.wait_ge(s_spread, g + 1)
                    if later(i) or ps.n:
                        dve.wait_ge(s_sum, g - 1)
                        dve.wait_ge(s_nw, g - 1)
                        dve.wait_ge(s_rank, AHALF * (g - 1))
                    for k in range(AHALF):
                        spread = ps_spread[h][:, k * P:(k + 1) * P]
                        own = cell[:, bass.ds(g * AHALF + k, 1)]
                        nc.vector.tensor_scalar(equal[:, h, k, :], spread, own, None, ALU.is_equal).then_inc(s_equal, 1)
                        nc.vector.scalar_tensor_tensor(out=earlier[:, h, k, :], in0=spread, scalar=own, in1=after[:, :],
                                                       op0=ALU.is_equal, op1=ALU.mult,
                                                       accum_out=rank[:, h, k:k + 1]).then_inc(s_rank, 1)

                def cells(i, h):
                    g = first + i * 2 + h
                    dve.wait_ge(s_rank, AHALF * (g + 1))
                    if later(i) or ps.n:
                        dve.wait_ge(s_acell, g - 1)
                    nc.vector.tensor_scalar(to_nowhere[:, h, :], rank[:, h, :], 0.0, nowhere[:, 0:1],
                                            ALU.is_gt, ALU.mult).then_inc(s_nw, 1)
                    dve.wait_ge(s_nw, g + 1)
                    if later(i) or ps.n:
                        dve.wait_ge(s_added, 16 * AHALF * (g - 1))
                    nc.vector.tensor_tensor(acell[:, h, :], to_nowhere[:, h, :], cell[:, bass.ds(g * AHALF, AHALF)],
                                            ALU.max).then_inc(s_acell, 1)

                def adds(i, h):
                    lo = (i * 2 + h) * HALF
                    _, offs = nc.values_load_multi_w_load_instructions(
                        ps.off[:, bass.ds(lo, HALF)], DVE_ONLY, min_val=0, max_val=(TILES - 1) * D,
                        skip_runtime_bounds_check_because="a chunk's tile is a count of at most TILES - 1 comparisons")
                    for k in range(HALF):
                        dest = acc[:, bass.ds(offs[k], D)]
                        dve.wait_ge(ps.prod, lo + k + 1)
                        if later(i) or h or k:
                            dve.wait_ge(ps.added, lo + k)
                        nc.vector.tensor_tensor(dest, psum[k][:, :], dest, ALU.add).then_inc(ps.added, 1)

                def body(i, columns):
                    if not later(i):
                        hots(0, 0)
                        compare(0, 0)
                        cells(0, 0)
                    part = DEGREE_TURNS.index(i) if ps.n and isinstance(i, int) and i in DEGREE_TURNS else None
                    for h in range(2):
                        after = after_half(i, h)
                        if after:
                            hots(*after)
                        if columns_at(ps.n, after, columns):
                            compare(*after)
                        adds(i, h)
                        if part is not None:
                            degrees(part * 2 + h, 2 * len(DEGREE_TURNS))
                        if ps.n and isinstance(i, int) and i == LOOPS - 1:
                            piece_lows(h + 1)
                        if columns_at(ps.n, after, columns):
                            cells(*after)
                loop_pass(dve, ps.n, body)
                dve.wait_ge(ps.added, CH)

            run_pass(passes[0])
            run_pass(passes[1])

            def statistics(lo, hi, base):
                for t in range(lo, hi):
                    dve.wait_ge(s_res, base + t + 1)
                    nc.vector.bn_stats(stats[:, t, :], acc[:, t * D:(t + 1) * D]).then_inc(s_bn, 1)
                for t in range(lo, hi):
                    dve.wait_ge(s_bn, base + t + 1)
                    nc.vector.bn_aggr(mv[:, t, :], stats[:, t, :]).then_inc(s_mv, 1)

            def scales(g, size, base_group):
                lo, hi = g * size, (g + 1) * size
                dve.wait_ge(s_sd, base_group + g + 1)
                link(nc.vector.reciprocal(rstd[:, 1, lo:hi], rstd[:, 0, lo:hi]))
                nc.vector.scalar_tensor_tensor(out=rstd[:, 2, lo:hi], in0=mv[:, lo:hi, 0], scalar=-1.0,
                                               in1=rstd[:, 1, lo:hi], op0=ALU.mult, op1=ALU.mult).then_inc(s_rs, 1)

            dve.wait_ge(s_dsq, 1)
            link(nc.vector.reciprocal(deg[:, 1, :], deg[:, 2, :]))
            link(nc.vector.scalar_tensor_tensor(out=dinv, in0=deg[:, 0, :], scalar=0.0, in1=deg[:, 1, :],
                                                op0=ALU.is_gt, op1=ALU.mult))
            def send(t):
                dve.wait_ge(s_c1, t + 1)
                nc.vector.tensor_scalar(rows(t), psum[2 + t % 2][:, 0:DH], dinv[:, t:t + 1],
                                        None, ALU.mult).then_inc(s_hs, 1)

            def lows(t, n):
                dve.wait_ge(s_hi, n * TILES + t + 1)
                nc.vector.tensor_tensor(low(t), rows(t), high[:, t, :].bitcast(F32), ALU.subtract).then_inc(s_lo, 1)

            for g in range(TILES // GROUP1):
                lo, hi = g * GROUP1, (g + 1) * GROUP1
                for t in range(lo, hi):
                    if t == TILES - 1:
                        dve.wait_ge(s_res, t - 3)
                        nc.vector.memset(xrow[64:P, t % 4], 0.0).then_inc(s_xz, 1)
                    dve.wait_ge(s_x[t % 4], 16 * (t // 4 + 1))
                    a = acc[:, t * D:(t + 1) * D]
                    nc.vector.scalar_tensor_tensor(out=a, in0=a, scalar=0.0, in1=xrow[:, t % 4],
                                                   op0=ALU.max, op1=ALU.add).then_inc(s_res, 1)
                    if t >= LEAD:
                        send(t - LEAD)
                        if t >= LEAD + 3:
                            lows(t - LEAD - 3, 0)
                        statistics(t, t + 1, 0)
                if lo < LEAD:
                    statistics(lo, hi, 0)
                scales(g, GROUP1, 0)
            for t in range(TILES - LEAD, TILES):
                send(t)
                lows(t - 3, 0)
            for t in range(TILES - 3, TILES):
                lows(t, 0)
            for t in range(TILES):
                piece_lows(AHEAD + PIECES * (t + 1) - (t == TILES - 1))
                z = rows(t)
                dve.wait_ge(s_piece, PIECES * (t + 1))
                nc.vector.tensor_tensor(z, psum[4 + t % 2][:, 0:DH], z, ALU.add).then_inc(s_z, 1)
                dve.wait_ge(s_z, 2 * t + 1)
                nc.vector.scalar_tensor_tensor(out=z, in0=z, scalar=dinv[:, t:t + 1], in1=b1s,
                                               op0=ALU.mult, op1=ALU.add).then_inc(s_z, 1)
                dve.wait_ge(s_z, 2 * t + 2)
                nc.vector.tensor_scalar(z, z, 0.0, dinv[:, t:t + 1], ALU.max, ALU.mult).then_inc(s_zz, 1)
            for t in range(TILES):
                lows(t, 1)
                if t == TILES // 2:
                    piece_lows(AHEAD + PIECES * TILES)
            for step in range(TILES + 2):
                upto = AHEAD + PIECES * (TILES + step + 1)
                piece_lows(upto - 1)
                if step < TILES:
                    dve.wait_ge(s_piece, PIECES * (TILES + step + 1))
                    if step >= 2:
                        dve.wait_ge(s_tp, TILES + step - 1)
                    nc.vector.tensor_tensor(conv2[:, step % 2, :], psum[4 + step % 2][:, 0:DH], rows(step),
                                            ALU.add).then_inc(s_last, 1)
                piece_lows(upto)
                t = step - 2
                if t < 0:
                    continue
                dve.wait_ge(s_c1, TILES + t + 1)
                if t >= YRING:
                    dve.wait_ge(s_sq, t - YRING + 1)
                    dve.wait_ge(s_res, TILES + t - YRING + 1)
                nc.vector.scalar_tensor_tensor(out=y[:, t % YRING, :], in0=psum[2 + t % 2][:, :],
                                               scalar=dinv[:, t:t + 1], in1=b2s,
                                               op0=ALU.mult, op1=ALU.add).then_inc(s_yv, 1)
                if t % GROUP2 != GROUP2 - 1:
                    continue
                g = t // GROUP2
                lo, hi = g * GROUP2, t + 1
                dve.wait_ge(s_sq, hi)
                nc.vector.tensor_scalar(cnt[:, 1, lo:hi], cnt[:, 0, lo:hi], TINY, None, ALU.max).then_inc(s_n1, 1)
                piece_lows(upto + 1)
                dve.wait_ge(s_n2, g + 1)
                link(nc.vector.tensor_scalar(cnt[:, 3, lo:hi], cnt[:, 2, lo:hi], EPS_NORM, None, ALU.max))
                link(nc.vector.reciprocal(cnt[:, 4, lo:hi], cnt[:, 3, lo:hi]))
                for tile in range(lo, hi):
                    a = acc[:, tile * D:(tile + 1) * D]
                    dve.wait_ge(s_yv, tile + 1)
                    nc.vector.scalar_tensor_tensor(out=a, in0=y[:, tile % YRING, :], scalar=cnt[:, 4, tile:tile + 1],
                                                   in1=a, op0=ALU.mult, op1=ALU.add).then_inc(s_res, 1)
                statistics(lo, hi, TILES)
                scales(g, GROUP2, TILES // GROUP1)

        @block.tensor
        def _(pe):
            for d in range(2):
                pe.wait_ge(s_cnt, d + 1)
                nc.tensor.matmul(ps_cnt[:, 0:TILES], before[:, :], cnt[:, 0, :], start=True, stop=True)
                nc.tensor.matmul(ps_cnt[:, 32:32 + TILES], ones[:, :], cnt[:, 0, :], start=True, stop=True).then_inc(s_tot, 1)

            pe.wait_ge(s_xT, 16)
            pe.wait_ge(s_dx, 1)
            pe.wait_ge(s_w[0], 32)
            for t in range(TILES):
                if t >= BANKS:
                    pe.wait_ge(s_hev, t - BANKS + 1)
                for k in range(KD):
                    mm = nc.tensor.matmul(psum[t % BANKS][:, :], xTs[:, k, t * P:(t + 1) * P], wbuf[:, 0, k, :],
                                          start=(k == 0), stop=(k == KD - 1))
                mm.then_inc(s_hmm, 1)

            def body(i):
                for h in range(2):
                    pe.wait_ge(s_w[1 - h], 32 * (i + 1 + h))
                    for t in range(TILES):
                        m = TILES + (i * 2 + h) * TILES + t
                        bank = (h * TILES + t) % BANKS
                        pe.wait_ge(s_hev, m - BANKS + 1)
                        for k in range(KD):
                            mm = nc.tensor.matmul(psum[bank][:, :], xTs[:, k, t * P:(t + 1) * P],
                                                  wbuf[:, 1 - h, k, :], start=(k == 0), stop=(k == KD - 1))
                        mm.then_inc(s_hmm, 1)
            loop(pe, R, body)
            pe.wait_ge(s_hev, (2 * R + 1) * TILES)

            def run_pass(ps):
                first = ps.n * HALVES

                def spread(i, h):
                    g = first + i * 2 + h
                    pe.wait_ge(s_diag, AHALF * (g + 1))
                    if later(i) or ps.n:
                        pe.wait_ge(s_asum, g - 1)
                    nc.tensor.matmul(ps_spread[h][:, 0:AHALF * P], ones[:, :],
                                     diag[:, h].rearrange("p k e -> p (k e)"), start=True, stop=True).then_inc(s_spread, 1)

                def sums(i, h):
                    g = first + i * 2 + h
                    pe.wait_ge(s_equal, AHALF * (g + 1))
                    pe.wait_ge(s_rank, AHALF * (g + 1))
                    for k in range(AHALF):
                        mm = nc.tensor.matmul(ps_spread[h][:, SUMS + k:SUMS + k + 1], equal[:, h, k, :],
                                              ew_f[:, bass.ds(g * AHALF + k, 1)], start=True, stop=True)
                    mm.then_inc(s_sum, 1)

                def body(i, columns):
                    if not later(i):
                        spread(0, 0)
                    for h in range(2):
                        if columns_at(ps.n, after_half(i, h), columns):
                            spread(*after_half(i, h))
                        if columns:
                            sums(i, h)
                        pe.wait_ge(ps.hot, i * 2 + h + 1)
                        if ps.degree and later(i):
                            pe.wait_ge(ps.dcol, i * 2 + h - 1)
                        for k in range(HALF):
                            slot = h * HALF + k
                            hot = onehot[:, h, k, :]
                            if later(i) or h:
                                pe.wait_ge(ps.added, i * SLOTS + slot - HALF + 1)
                            pe.wait_ge(ps.got[slot], 16 * (i + 1))
                            if ps.degree:
                                nc.tensor.matmul(ps_deg[h][:, k:k + 1], hot,
                                                 list0[:, bass.ds(i * SLOTS + slot, 1), 2:3].rearrange("p a b -> p (a b)"),
                                                 start=True, stop=True)
                            nc.tensor.matmul(psum[k][:, :], hot, gathered[:, slot, :],
                                             start=True, stop=True).then_inc(ps.prod, 1)
                loop_pass(pe, ps.n, body)

            pe.wait_ge(s_cell, 1)
            run_pass(passes[0])
            run_pass(passes[1])

            def convolve(n, t):
                m = n * TILES + t
                if m >= 2:
                    pe.wait_ge(*((s_z, 2 * m - 3) if m - 2 < TILES else (s_last, m - 1 - TILES)))
                for part in range(PIECES):
                    j = m * PIECES + part
                    pe.wait_ge(s_ml, j + 1)
                    for k in range(PBLOCKS):
                        block = part * PBLOCKS + k
                        if t == 0:
                            pe.wait_ge(s_lo, n * TILES + block + 1)
                        hi, lo = piece_hi[:, j % HIGHS, k * P:(k + 1) * P], piece_lo[:, j % RAWS, k * P:(k + 1) * P]
                        rows_hi, rows_lo = high[:, block, :], low(block)
                        into = psum[4 + t % 2][:, 0:DH]
                        nc.tensor.matmul(into, hi, rows_hi, start=(block == 0), stop=False)
                        nc.tensor.matmul(into, hi, rows_lo, start=False, stop=False)
                        mm = nc.tensor.matmul(into, lo, rows_hi, start=False, stop=(block == TILES - 1))
                    mm.then_inc(s_piece, 1)

            def transposes(source, blocks, t, base):
                if base + t >= 2:
                    pe.wait_ge(s_tpc, base + t - 1)
                for k in range(blocks):
                    mm = nc.tensor.transpose(psum[t % 2][:, k * P:(k + 1) * P], source[:, k * P:(k + 1) * P], ident[:, :])
                mm.then_inc(s_tp, 1)

            def multiply(blocks, weight, width, t, base):
                pe.wait_ge(s_tpc, base + t + 1)
                for k in range(blocks):
                    mm = nc.tensor.matmul(psum[2 + t % 2][:, 0:width], xt1[:, t % 2, k * P:(k + 1) * P],
                                          weight[:, k, :], start=(k == 0), stop=(k == blocks - 1))
                mm.then_inc(s_c1, 1)

            pe.wait_ge(s_b12, 64)
            pe.wait_ge(passes[1].added, CH)
            for t in range(TILES + 1):
                if t < TILES:
                    pe.wait_ge(s_x1, t + 1)
                    transposes(acc[:, t * D:(t + 1) * D], KD, t, 0)
                if t:
                    if t >= 3:
                        pe.wait_ge(s_hs, t - 2)
                    multiply(KD, w1s, DH, t - 1, 0)
            for t in range(TILES):
                convolve(0, t)
            for t in range(TILES + 2):
                if t < TILES:
                    convolve(1, t)
                if 0 < t <= TILES:
                    pe.wait_ge(s_last, t)
                    transposes(conv2[:, (t - 1) % 2, :], KH, t - 1, TILES)
                if t >= 2:
                    if t >= 4:
                        pe.wait_ge(s_yv, t - 3)
                    multiply(KH, w2s, D, t - 2, TILES)


def kernel(**inputs):
    import numpy as _np
    import concourse.bacc as _bacc
    from concourse import mybir as _mybir
    from concourse.bass_utils import run_bass_kernel_spmd as _run

    given = {k: _np.asarray(v) for k, v in inputs.items()}
    laid = [
        ("x", given["x"]), ("xT", given["x"].T),
        ("src", given["src"]), ("dst", given["dst"]), ("rel", given["edge_type_8"]), ("ew", given["edge_weight"]),
        ("wselfT", given["L0_gnn_W_self"].T), ("bself", given["L0_gnn_b_self"]),
        ("wrelT", _np.roll(given["L0_gnn_W_rel"], R, axis=0).transpose(0, 2, 1)),
        ("brel", _np.roll(given["L0_gnn_b_rel"], R, axis=0)),
        ("w1", given["L1_gnn_W1"]), ("b1", given["L1_gnn_b1"]),
        ("w2", given["L1_gnn_W2"]), ("b2", given["L1_gnn_b2"]),
    ]
    nc = _bacc.Bacc("TRN2", target_bir_lowering=False, num_devices=1)
    arrays, args = {}, []
    for name, a in laid:
        a = _np.ascontiguousarray(a)
        arrays[f"in_{name}_dram"] = a
        args.append(nc.dram_tensor(f"in_{name}_dram", a.shape, _mybir.dt.from_np(a.dtype), kind="ExternalInput").ap())
    args.append(nc.dram_tensor("out_0_dram", (N, D), _mybir.dt.float32, kind="ExternalOutput").ap())
    build(nc, *args)
    r = _run(nc, [arrays], core_ids=[0])
    return r.results[0]["out_0_dram"]
```
